# Optimizing a Trainium2 kernel written in Bass

```python
import numpy as np
import jax
import jax.numpy as jnp

def _softmax(x, axis=-1):
    return jax.nn.softmax(x, axis=axis)

def _gelu(x):
    return jax.nn.gelu(x, approximate=True)

def _silu(x):
    return jax.nn.silu(x)

def _sigmoid(x):
    return jax.nn.sigmoid(x)

def _layernorm(x, axis=-1, eps=1e-05):
    m = jnp.mean(x, axis=axis, keepdims=True)
    v = jnp.var(x, axis=axis, keepdims=True)
    return (x - m) / jnp.sqrt(v + eps)

def _scatter_add(tgt, idx, src, axis=0):
    return tgt.at[idx].add(src)

def _segment_sum(src, seg, n):
    return jax.ops.segment_sum(src, seg, n)
kernel_name = 'mk_macaron_d1_jaxref_r4_a3cb0b'

def setup_inputs(seed: int=0):
    np.random.seed(seed)
    _w = jnp.asarray

    def _L0_attn_setup():
        import jax, jax.numpy as jnp
        import numpy as np
        N_EMBD = 256
        N_HEAD = 16
        LATENT = 64
        HEAD_DIM = N_EMBD // N_HEAD
        B, T = (2, 512)
        SCALE = 1.0 / np.sqrt(LATENT)
        key = jax.random.key(seed)
        ks = jax.random.split(key, 10)
        s = lambda fan_in: 1.0 / np.sqrt(fan_in)
        return {'x': jax.random.normal(ks[0], (B, T, N_EMBD), dtype=jnp.float32), 'Wq': jax.random.normal(ks[1], (N_EMBD, N_EMBD), dtype=jnp.float32) * s(N_EMBD), 'bq': jnp.zeros((N_EMBD,), dtype=jnp.float32), 'Wk': jax.random.normal(ks[2], (N_EMBD, N_HEAD * LATENT), dtype=jnp.float32) * s(N_EMBD), 'bk': jnp.zeros((N_HEAD * LATENT,), dtype=jnp.float32), 'Wv': jax.random.normal(ks[3], (N_EMBD, N_HEAD * LATENT), dtype=jnp.float32) * s(N_EMBD), 'bv': jnp.zeros((N_HEAD * LATENT,), dtype=jnp.float32), 'Wo': jax.random.normal(ks[4], (N_HEAD * LATENT, N_EMBD), dtype=jnp.float32) * s(N_HEAD * LATENT), 'bo': jnp.zeros((N_EMBD,), dtype=jnp.float32), 'Wc': jax.random.normal(ks[5], (HEAD_DIM, LATENT), dtype=jnp.float32) * s(HEAD_DIM)}
    _L0_attn_in = _L0_attn_setup()

    def _L0_ffn_setup():
        import jax, jax.numpy as jnp
        import numpy as np
        DIM = 256

        def _reference_tuple_inner(x, W_r, W_k, W_v, mu_r, mu_k):
            B, T, C = x.shape
            x_prev = jnp.concatenate([jnp.zeros((B, 1, C), x.dtype), x[:, :-1, :]], axis=1)
            xr = mu_r * x + (1.0 - mu_r) * x_prev
            xk = mu_k * x + (1.0 - mu_k) * x_prev
            r = jax.nn.sigmoid(jnp.einsum('btc,dc->btd', xr, W_r))
            k = jnp.einsum('btc,dc->btd', xk, W_k)
            k_act = jnp.square(jax.nn.relu(k))
            out = r * jnp.einsum('btc,dc->btd', k_act, W_v)
            new_state = x[:, -1, :]
            return (out, new_state)
        key = jax.random.key(seed)
        ks = jax.random.split(key, 6)
        B, T, C = (8, 512, DIM)
        x = jax.random.normal(ks[0], (B, T, C), dtype=jnp.float32)
        s = 1.0 / np.sqrt(C)
        W_r = jax.random.uniform(ks[1], (C, C), jnp.float32, -s, s)
        W_k = jax.random.uniform(ks[2], (C, C), jnp.float32, -s, s)
        W_v = jax.random.uniform(ks[3], (C, C), jnp.float32, -s, s)
        mu_r = jax.random.uniform(ks[4], (C,), jnp.float32)
        mu_k = jax.random.uniform(ks[5], (C,), jnp.float32)
        return {'x': x, 'W_r': W_r, 'W_k': W_k, 'W_v': W_v, 'mu_r': mu_r, 'mu_k': mu_k}
    _L0_ffn_in = _L0_ffn_setup()
    _d = {'L0_attn_x': _L0_attn_in['x'], 'L0_attn_Wq': _L0_attn_in['Wq'], 'L0_attn_bq': _L0_attn_in['bq'], 'L0_attn_Wk': _L0_attn_in['Wk'], 'L0_attn_bk': _L0_attn_in['bk'], 'L0_attn_Wv': _L0_attn_in['Wv'], 'L0_attn_bv': _L0_attn_in['bv'], 'L0_attn_Wo': _L0_attn_in['Wo'], 'L0_attn_bo': _L0_attn_in['bo'], 'L0_attn_Wc': _L0_attn_in['Wc'], 'L0_ffn_W_r': _L0_ffn_in['W_r'], 'L0_ffn_W_k': _L0_ffn_in['W_k'], 'L0_ffn_W_v': _L0_ffn_in['W_v'], 'L0_ffn_mu_r': _L0_ffn_in['mu_r'], 'L0_ffn_mu_k': _L0_ffn_in['mu_k']}
    _x0 = _d['L0_attn_x']
    _d['L0_attn_x'] = jax.random.normal(jax.random.fold_in(jax.random.key(seed), 1), (2, 2048, 256), dtype=_x0.dtype)
    del _x0
    return _d

def reference(L0_attn_x, L0_attn_Wq, L0_attn_bq, L0_attn_Wk, L0_attn_bk, L0_attn_Wv, L0_attn_bv, L0_attn_Wo, L0_attn_bo, L0_attn_Wc, L0_ffn_W_r, L0_ffn_W_k, L0_ffn_W_v, L0_ffn_mu_r, L0_ffn_mu_k):

    def _L0_attn_ref(x, Wq, bq, Wk, bk, Wv, bv, Wo, bo, Wc):
        import jax, jax.numpy as jnp
        import numpy as np
        N_EMBD = 256
        N_HEAD = 16
        LATENT = 64
        HEAD_DIM = N_EMBD // N_HEAD
        B, T = (2, 512)
        SCALE = 1.0 / np.sqrt(LATENT)
        Bv, Tv, C = x.shape
        q = (x @ Wq + bq).reshape(Bv, Tv, N_HEAD, HEAD_DIM)
        k = (x @ Wk + bk).reshape(Bv, Tv, N_HEAD, LATENT)
        v = (x @ Wv + bv).reshape(Bv, Tv, N_HEAD, LATENT)
        qc = jnp.einsum('bthd,dl->bthl', q, Wc)
        att = jnp.einsum('bthl,bshl->bhts', qc, k) * SCALE
        causal = jnp.tril(jnp.ones((Tv, Tv), dtype=bool))
        att = jnp.where(causal[None, None], att, -jnp.inf)
        att = jax.nn.softmax(att, axis=-1)
        y = jnp.einsum('bhts,bshl->bthl', att, v).reshape(Bv, Tv, N_HEAD * LATENT)
        return y @ Wo + bo

    def _L0_ffn_ref(x, W_r, W_k, W_v, mu_r, mu_k):
        import jax, jax.numpy as jnp
        import numpy as np
        DIM = 256

        def _reference_tuple_inner(x, W_r, W_k, W_v, mu_r, mu_k):
            B, T, C = x.shape
            x_prev = jnp.concatenate([jnp.zeros((B, 1, C), x.dtype), x[:, :-1, :]], axis=1)
            xr = mu_r * x + (1.0 - mu_r) * x_prev
            xk = mu_k * x + (1.0 - mu_k) * x_prev
            r = jax.nn.sigmoid(jnp.einsum('btc,dc->btd', xr, W_r))
            k = jnp.einsum('btc,dc->btd', xk, W_k)
            k_act = jnp.square(jax.nn.relu(k))
            out = r * jnp.einsum('btc,dc->btd', k_act, W_v)
            new_state = x[:, -1, :]
            return (out, new_state)
        return _reference_tuple_inner(x, W_r, W_k, W_v, mu_r, mu_k)[0]
    x = L0_attn_x
    x = x + 0.5 * _L0_ffn_ref(_layernorm(x, axis=-1), L0_ffn_W_r, L0_ffn_W_k, L0_ffn_W_v, L0_ffn_mu_r, L0_ffn_mu_k)
    x = x + _L0_attn_ref(_layernorm(x, axis=-1), L0_attn_Wq, L0_attn_bq, L0_attn_Wk, L0_attn_bk, L0_attn_Wv, L0_attn_bv, L0_attn_Wo, L0_attn_bo, L0_attn_Wc)
    x = x + 0.5 * _L0_ffn_ref(_layernorm(x, axis=-1), L0_ffn_W_r, L0_ffn_W_k, L0_ffn_W_v, L0_ffn_mu_r, L0_ffn_mu_k)
    return x

_drawn_inputs = setup_inputs


def setup_inputs(seed=0):
    import zlib

    import numpy as np

    out = dict(_drawn_inputs(seed))
    spreads = {'L0_attn_bq': (0.0, 0.8),
     'L0_attn_bk': (0.0, 0.8),
     'L0_attn_bv': (0.0, 0.1),
     'L0_attn_bo': (0.0, 0.1)}
    factors = {'L0_ffn_W_r': 3.215, 'L0_ffn_mu_r': 6.497}
    for name, (base, spread) in spreads.items():
        noise = np.random.default_rng([zlib.crc32(name.encode()), seed]).standard_normal(out[name].shape)
        drawn = base * np.exp(spread * noise) if base else spread * noise
        out[name] = jnp.asarray(drawn.astype(out[name].dtype))
    for name, factor in factors.items():
        out[name] = (out[name] * factor).astype(out[name].dtype)
    return out
```

```python
import concourse.bass as bass
from concourse import mybir
from contextlib import ExitStack


def macaron_block(nc, x, out, ffn_wr, ffn_wk, ffn_wv, mu_r, mu_k, wq, bq, wk_t, bk, wc_t, wv, bv, wo, bo,
                  qk_scratch, shift_scratch, den_scratch, rden_scratch):
    fp32, bf16, i32 = mybir.dt.float32, mybir.dt.bfloat16, mybir.dt.int32
    ALU, ACT, AX = mybir.AluOpType, mybir.ActivationFunctionType, mybir.AxisListType

    P = 128
    C = wq.shape[2]
    BATCH = qk_scratch.shape[0]
    T = x.shape[0] // BATCH
    KT = C // P
    CH = 512
    NCH = T // CH
    BPC = CH // P
    NBLK = T // P
    HEADS, LAT = 16, 64
    HD = C // HEADS
    PAIRS = HEADS // 2
    PRODUCTS = ((0, 0), (0, 1), (0, 2), (1, 0), (1, 1), (2, 0))
    QROWS = len(PRODUCTS) * HD + 1
    SCALE = LAT ** -0.5
    EPS = 1e-5
    SAFE = 35.0 / SCALE
    MARGIN = 1.01
    MASKED = -3.0e38

    UNITS = []
    for c in range(NCH):
        UNITS += [(c, j, 0, False) for j in range(BPC * c)]
        UNITS += [(c, BPC * c + i, P * i, True) for i in range(BPC)]
    NU = len(UNITS)
    FIRST = [u for u in range(NU) if u == 0 or UNITS[u - 1][0] != UNITS[u][0]]
    LAST = [u for u in range(NU) if u == NU - 1 or UNITS[u + 1][0] != UNITS[u][0]]
    DIAG = [sum(UNITS[v][3] for v in range(u)) for u in range(NU)]
    NDIAG = NCH * BPC
    NP_BUF = 4
    PV_LAG = 3
    GROUPS = NCH // 2
    assert NU % NP_BUF == 0 and NU % 2 == 0

    ctx = ExitStack()
    with ctx:
        def sb(name, shape, dt=fp32):
            return ctx.enter_context(nc.sbuf_tensor(name, shape, dt))

        def sem(name):
            return ctx.enter_context(nc.semaphore(name))

        w_r, w_k, w_v = sb("w_r", [P, KT, C]), sb("w_k", [P, KT, C]), sb("w_v", [P, KT, C])
        mur, muk = sb("mur", [P, KT]), sb("muk", [P, KT])
        w_q, b_q = sb("w_q", [P, KT, C]), sb("b_q", [P, KT])
        w_kc, b_kc = sb("w_kc", [P, KT, C]), sb("b_kc", [P, KT])
        w_val, b_val = sb("w_val", [P, KT, HEADS * LAT]), sb("b_val", [P, HEADS * LAT])
        w_o, b_o = sb("w_o", [P, PAIRS, C]), sb("b_o", [P, C])
        b_k_raw = sb("b_k_raw", [P, PAIRS])
        wc_pair = sb("wc_pair", [P, 2 * HD])
        ident = sb("ident", [P, P])
        ones = sb("ones", [P, 32])
        head_rows = sb("head_rows", [P, KT, HEADS], bf16)
        eps_half = sb("eps_half", [P, BPC])
        tri = sb("tri", [P, P])

        x_sb = sb("x_sb", [P, NBLK, C])
        slots = sb("slots", [P, PAIRS, NBLK * P])
        stats = sb("stats", [P, 2, BPC, 6])
        mv = sb("mv", [P, 2, BPC, 2])
        rstd = sb("rstd", [P, 2, BPC])
        kmax4, kmax, over = sb("kmax4", [HEADS, NCH]), sb("kmax", [HEADS, 1]), sb("over", [HEADS, 1])
        flag = sb("flag", [1, 1], i32)

        qs = [sb(f"qs{i}", [P, 2, T], bf16) for i in range(2)]
        ks = [sb(f"ks{i}", [P, 2, T], bf16) for i in range(2)]
        vb = [sb(f"vb{i}", [P, NBLK, P]) for i in range(2)]
        probs = [sb(f"probs{i}", [P, 2, CH]) for i in range(NP_BUF)]
        acc = [sb(f"acc{i}", [P, 2, CH]) for i in range(NCH)]
        den = sb("den", [P, GROUPS, CH])
        den_c, rden_c = sb("den_c", [P, 2 * T // P]), sb("rden_c", [P, 2 * T // P])
        rden = sb("rden", [P, NCH, CH])

        def view(t, k, n, shape):
            flat = t[:].rearrange("p a b -> p (a b)")[:, 2 * k:2 * (k + n)].bitcast(fp32)
            return flat.rearrange("p (a b) -> p a b", a=shape[0])
        W = CH * KT
        xn = [view(qs[0], i * W, W, (BPC, C)) for i in range(2)]
        x_r = [view(qs[1], i * W, W, (KT, CH)) for i in range(2)]
        x_k = [view(ks[0], i * W, W, (KT, CH)) for i in range(2)]
        diff = view(ks[1], 0, W, (KT, CH))
        prod = view(ks[1], W, W, (BPC, C))
        kact = [probs[i] for i in range(2)]
        gate = [probs[2 + i][:].rearrange("p a (b c) -> p (a b) c", b=BPC // KT) for i in range(2)]
        xnt = [vb[i][:].rearrange("p a b -> p (a b)")[:, 0:KT * (CH + 2)].rearrange("p (a b) -> p a b", a=KT)
               for i in range(2)]
        qf, kf = view(qs[1], 0, W, (KT, CH)), view(qs[1], W, W, (KT, CH))
        q_parts = ks[0][:].rearrange("p a b -> p (a b)")[:, 0:3 * W].rearrange("p (s a b) -> p s a b", s=3, a=KT)
        k_parts = ks[1][:].rearrange("p a b -> p (a b)")[:, 0:3 * W].rearrange("p (s a b) -> p s a b", s=3, a=KT)
        rest = [probs[0], probs[1]]
        sq = [probs[2 + i][:].rearrange("p a b -> p (a b)")[:, 0:W // 2].bitcast(bf16)
              .rearrange("p (a b) -> p a b", a=KT) for i in range(2)]
        qnorm = rden[0:HEADS].rearrange("p a b -> p (a b)")
        shift = den[0:HEADS].rearrange("p a b -> p (a b)").bitcast(bf16)
        wk_raw = slots[:].rearrange("p a b -> p (a b)")[:, 0:PAIRS * C].rearrange("p (a b) -> p a b", a=PAIRS)

        pa, pb, pc, pd = (ctx.enter_context(nc.psum_tensor(n, [P, 2, CH], fp32)) for n in ("pa", "pb", "pc", "pd"))
        scores = [pa, pb]
        banks = [t[:, i, :] for t in (pa, pb, pc, pd) for i in range(2)]

        w_loaded, wc_zeroed, wc_loaded, wk_loaded = sem("w_loaded"), sem("wc_zeroed"), sem("wc_loaded"), sem("wk_loaded")
        consts_set, ident_set, kc_done, kc_copied = sem("consts_set"), sem("ident_set"), sem("kc_done"), sem("kc_copied")
        x_loaded = [sem(f"x_loaded{c}") for c in range(NCH)]
        out_stored = [sem(f"out_stored{c}") for c in range(NCH)]
        dve_step, waited = sem("dve_step"), sem("waited")
        stats_ready, rstd_ready, xn_ready = sem("stats_ready"), sem("rstd_ready"), sem("xn_ready")
        pool_step = sem("pool_step")
        xnt_made, xnt_copied = sem("xnt_made"), sem("xnt_copied")
        mixed = sem("mixed")
        gate_made, gate_ready = sem("gate_made"), sem("gate_ready")
        k_made, k_relu, kact_ready = sem("k_made"), sem("k_relu"), sem("kact_ready")
        ffn_made, ffn_read, ffn_added = sem("ffn_made"), sem("ffn_read"), sem("ffn_added")
        q_made, kp_made, v_made = sem("q_made"), sem("kp_made"), sem("v_made")
        q_copied, kp_copied, squares = sem("q_copied"), sem("kp_copied"), sem("squares")
        v_stored, q_split, k_split = sem("v_stored"), sem("q_split"), sem("k_split")
        q_saved, k_saved = sem("q_saved"), sem("k_saved")
        norms_made, norms_read = sem("norms_made"), sem("norms_read")
        bound_inputs, bound_ready, shift_ready, shift_saved = (
            sem("bound_inputs"), sem("bound_ready"), sem("shift_ready"), sem("shift_saved"))
        over_ready, over_counted, flag_ready = sem("over_ready"), sem("over_counted"), sem("flag_ready")
        pair_loaded = [sem(f"pair_loaded{i}") for i in range(2)]
        ones_rows = sem("ones_rows")
        scored, exped, masked, summed, valued = sem("scored"), sem("exped"), sem("masked"), sem("summed"), sem("valued")
        y_copied, den_made, den_copied = sem("y_copied"), sem("den_made"), sem("den_copied")
        den_sent, den_back, rden_made, rden_sent, rden_back = (
            sem("den_sent"), sem("den_back"), sem("rden_made"), sem("rden_sent"), sem("rden_back"))
        y_scaled, bo_added, o_made, o_added = sem("y_scaled"), sem("bo_added"), sem("o_made"), sem("o_added")
        g_loaded, g_scored, g_read, g_max, g_sent, g_step = (
            sem("g_loaded"), sem("g_scored"), sem("g_read"), sem("g_max"), sem("g_sent"), sem("g_step"))

        LN_TURNS, FFN_TURNS, VT = 3 * NCH, 2 * NCH, BPC * 2

        def ln(b, st, c):
            return b * LN_TURNS + (st * NCH + c)

        def ff(b, w, c):
            return b * FFN_TURNS + (w * NCH + c)

        def wait_alone(eng, s, count):
            eng.wait_ge(s, count)
            eng.sem_inc(waited, 1)

        G_TURNS, G_STEPS = 2 * NBLK, 4
        g_part = sb("g_part", [P, NCH + 1])
        g_diag = probs[0][:, 0, 0:P]
        g_top = sb("g_top", [P, 1])
        g_shift = sb("g_shift", [P, 2, NBLK], bf16)

        def g_turn(b, p, i):
            return (b * PAIRS + p) * G_TURNS + i

        block = ctx.enter_context(nc.Block())

        @block.sync
        def _(sp):
            for s in (q_saved, k_saved, den_sent, g_sent, *out_stored):
                sp.sem_inc(s, 16)
            sp.dma_start(wk_raw, wk_t).then_inc(wk_loaded, 16)
            sp.dma_start(b_k_raw[:], bk).then_inc(wk_loaded, 16)
            sp.wait_ge(wc_zeroed, 1)
            for i in range(2):
                sp.dma_start(wc_pair[i * LAT:(i + 1) * LAT, i * HD:(i + 1) * HD], wc_t).then_inc(wc_loaded, 16)
            for dst, src in ((w_r, ffn_wr), (w_k, ffn_wk), (w_v, ffn_wv), (mur, mu_r), (muk, mu_k), (w_q, wq),
                             (b_q, bq), (w_val, wv), (w_o, wo)):
                sp.dma_start(dst[:], src).then_inc(w_loaded, 16)
            sp.dma_start(b_val[:], bv.to_broadcast([P, HEADS * LAT])).then_inc(w_loaded, 16)
            sp.dma_start(b_o[:], bo.to_broadcast([P, C])).then_inc(w_loaded, 16)

            def part_rows(b, p, what, part):
                src = qk_scratch[b, what, part, bass.ds(p * (2 * HD), 2 * HD), :]
                return src.rearrange("(h d) t -> d h t", h=2)

            def load_pair(b, p, par):
                for s, (qp, kp) in enumerate(PRODUCTS):
                    rows = slice(s * HD, (s + 1) * HD)
                    sp.dma_start(qs[par][rows, :, :], part_rows(b, p, 0, qp)).then_inc(pair_loaded[par], 16)
                    sp.dma_start(ks[par][rows, :, :], part_rows(b, p, 1, kp)).then_inc(pair_loaded[par], 16)
                src = shift_scratch[b, bass.ds(p * 2, 2), :].rearrange("(o h) t -> o h t", o=1)
                sp.dma_start(qs[par][QROWS - 1:QROWS, :, :], src).then_inc(pair_loaded[par], 16)
                sp.dma_start(vb[par][:].rearrange("p a b -> p (a b)"),
                             slots[:, bass.ds(p, 1), :].rearrange("p o n -> p (o n)")).then_inc(pair_loaded[par], 16)

            def reciprocals(n):
                for g in range(GROUPS):
                    sp.wait_ge(den_copied, n * GROUPS + (2 + g + 1))
                    sp.dma_start(den_scratch[g], den[0:P:32, g, :]).then_inc(den_sent, 16)
                sp.wait_ge(den_sent, n * (16 * GROUPS) + 16 * GROUPS + 16)
                sp.dma_start(den_c[:], den_scratch.rearrange("g r (a c) -> (g r a) c", c=2 * T // P)).then_inc(den_back, 16)
                sp.wait_ge(rden_made, n + 1)
                sp.dma_start(rden_scratch.rearrange("g r (a c) -> (g r a) c", c=2 * T // P), rden_c[:]).then_inc(rden_sent, 16)
                sp.wait_ge(rden_sent, n * 16 + 16)
                sp.wait_ge(y_scaled, n + 1)
                for h in range(2):
                    src = rden_scratch.rearrange("g (c h) n -> h (g c) n", h=2)[h:h + 1]
                    sp.dma_start(rden[h * LAT:(h + 1) * LAT, :, :],
                                 src.to_broadcast([LAT, NCH, CH])).then_inc(rden_back, 16)

            with sp.Fori(0, BATCH) as b:
                for c in range(NCH):
                    sp.wait_ge(out_stored[c], b * 16 + 16)
                    if c == 0:
                        pass
                    rows = x[bass.ds(b * T + c * CH, CH), :].rearrange("(n p) c -> p n c", p=P)
                    sp.dma_start(x_sb[:, c * BPC:(c + 1) * BPC, :], rows).then_inc(x_loaded[c], 16)
                for c in range(NCH):
                    for what, parts, split, saved in ((0, q_parts, q_split, q_saved), (1, k_parts, k_split, k_saved)):
                        sp.wait_ge(split, b * NCH + (c + 1))
                        dst = qk_scratch[b, what, :, :, c * CH:(c + 1) * CH].rearrange("s (f p) t -> p (s f) t", p=P)
                        sp.dma_start(dst, parts.rearrange("p s f t -> p (s f) t")).then_inc(saved, 16)
                sp.wait_ge(shift_ready, b + 1)
                sp.dma_start(shift_scratch[b], shift).then_inc(shift_saved, 16)
                wait_alone(sp, q_saved, b * (16 * NCH) + 16 * NCH + 16)
                wait_alone(sp, k_saved, b * (16 * NCH) + 16 * NCH + 16)
                wait_alone(sp, shift_saved, b * 16 + 16)
                wait_alone(sp, v_stored, b * (NCH * VT) + NCH * VT)
                wait_alone(sp, valued, b * (PAIRS * NU) + NP_BUF)
                wait_alone(sp, flag_ready, b + 1)
                general = sp.value_load(flag[0:1, 0:1], min_val=0, max_val=HEADS)
                with sp.If(general > 0):
                    with sp.Fori(0, PAIRS) as p:
                        for s, (qp, kp) in enumerate(PRODUCTS):
                            rows = slice(s * HD, (s + 1) * HD)
                            sp.dma_start(qs[0][rows, :, :], part_rows(b, p, 0, qp)).then_inc(g_loaded, 16)
                            sp.dma_start(ks[0][rows, :, :], part_rows(b, p, 1, kp)).then_inc(g_loaded, 16)
                        sp.wait_ge(g_max, b * PAIRS + p + 1)
                        dst = shift_scratch[b, bass.ds(p * 2, 2), :].rearrange("h (n p) -> p h n", p=P)
                        with nc.allow_non_contiguous_dma(reason="a column of maxima becomes a row"):
                            sp.dma_start(dst, g_shift[:]).then_inc(g_sent, 16)
                        wait_alone(sp, g_sent, (b * PAIRS + p) * 16 + 32)
                with sp.Else():
                    sp.sem_inc(g_loaded, PAIRS * len(PRODUCTS) * 32)
                    sp.sem_inc(g_sent, PAIRS * 16)
                for par in range(2):
                    load_pair(b, par, par)
                with sp.Fori(0, PAIRS // 2) as pp:
                    for par in range(2):
                        n = b * PAIRS + pp * 2 + par
                        wait_alone(sp, valued, n * NU + (NU + NP_BUF))
                        with sp.If(pp < PAIRS // 2 - 1):
                            later = nc.s_assert_within(pp * 2 + (par + 2), 0, PAIRS - 1,
                                                       skip_runtime_bounds_check_because="the last turn is left out")
                            load_pair(b, later, par)
                        reciprocals(n)
                for c in range(NCH):
                    sp.wait_ge(ffn_added, ff(b, 1, c) + 1)
                    rows = out[bass.ds(b * T + c * CH, CH), :].rearrange("(n p) c -> p n c", p=P)
                    sp.dma_start(rows, x_sb[:, c * BPC:(c + 1) * BPC, :]).then_inc(out_stored[c], 16)
            for c in range(NCH):
                sp.wait_ge(out_stored[c], 16 * BATCH + 16)
            sp.wait_ge(rden_back, 32 * PAIRS * BATCH)

        @block.tensor
        def _(pe):
            mm = nc.tensor.matmul

            def transposes(b, st, c):
                pe.wait_ge(xn_ready, ln(b, st, c) + 1)
                pe.wait_ge(xnt_copied, ln(b, st, c) + 1)
                if st == 2 and c == 0:
                    pe.wait_ge(o_added, b * NBLK + (NBLK - 6))
                for ft in range(KT):
                    for i in range(BPC):
                        last = nc.tensor.transpose(pa[:, ft, i * P:(i + 1) * P], xn[c % 2][:, i, ft * P:(ft + 1) * P],
                                                   ident[:])
                last.then_inc(xnt_made, 1)

            def ffn(b, w):
                st = 2 * w
                transposes(b, st, 0)
                for c in range(NCH):
                    pe.wait_ge(mixed, ff(b, w, c) + 1 + 1)
                    pe.wait_ge(gate_ready, ff(b, w, c) + 1)
                    if w == 1 and c == 0:
                        pe.wait_ge(o_added, b * NBLK + (NBLK - 2))
                    for i in range(BPC):
                        for kt in range(KT):
                            last = mm(pc[:, i // 2, (i % 2) * C:(i % 2 + 1) * C], x_r[c % 2][:, kt, i * P:(i + 1) * P],
                                      w_r[:, kt, :], start=kt == 0, stop=kt == KT - 1)
                    last.then_inc(gate_made, 1)
                    pe.wait_ge(k_relu, ff(b, w, c) + 1)
                    for mt in range(KT):
                        for kt in range(KT):
                            last = mm(pb[:, mt, :], w_k[:, kt, mt * P:(mt + 1) * P], x_k[c % 2][:, kt, :],
                                      start=kt == 0, stop=kt == KT - 1)
                    last.then_inc(k_made, 1)
                    if c + 1 < NCH:
                        transposes(b, st, c + 1)
                    pe.wait_ge(kact_ready, ff(b, w, c) + 1)
                    pe.wait_ge(ffn_read, ff(b, w, c) + 1)
                    if w == 1 and c == 0:
                        pe.wait_ge(o_added, b * NBLK + NBLK)
                    for i in range(BPC):
                        for kt in range(KT):
                            last = mm(pd[:, i // 2, (i % 2) * C:(i % 2 + 1) * C], kact[c % 2][:, kt, i * P:(i + 1) * P],
                                      w_v[:, kt, :], start=kt == 0, stop=kt == KT - 1)
                    last.then_inc(ffn_made, 1)

            def projections(b):
                transposes(b, 1, 0)
                for c in range(NCH):
                    turn = b * NCH + c
                    pe.wait_ge(xnt_copied, ln(b, 1, c) + 1 + 1)
                    if c == 0:
                        pe.wait_ge(k_relu, ff(b, 0, NCH - 1) + 1 + 1)
                        pe.wait_ge(gate_ready, ff(b, 0, NCH - 1) + 1 + 1)
                        pe.wait_ge(ffn_read, ff(b, 0, NCH - 1) + 1 + 1)
                    else:
                        pe.wait_ge(norms_read, turn)
                    xt = xnt[c % 2][:, :, 1:CH + 1]
                    for dst, wt, made in ((pb, w_q, q_made), (pc, w_kc, kp_made)):
                        if dst is pc and c > 0:
                            pe.wait_ge(kp_copied, turn)
                        for mt in range(KT):
                            for kt in range(KT):
                                last = mm(dst[:, mt, :], wt[:, kt, mt * P:(mt + 1) * P], xt[:, kt, :],
                                          start=kt == 0, stop=kt == KT - 1)
                        last.then_inc(made, 1)
                    for i in range(VT):
                        if i == VT // 2 and c + 1 < NCH:
                            transposes(b, 1, c + 1)
                        if c > 0 or i > 1:
                            pe.wait_ge(v_stored, turn * VT + (i - 1))
                        blk, half = i // 2, i % 2
                        for kt in range(KT):
                            last = mm(pd[:, i % 2, :], xt[:, kt, blk * P:(blk + 1) * P],
                                      w_val[:, kt, half * CH:(half + 1) * CH], start=kt == 0, stop=kt == KT - 1)
                        last.then_inc(v_made, 1)
                    pe.wait_ge(squares, turn * 2 + 2)
                    for what in range(2):
                        for ft in range(KT):
                            last = mm(pb[0:HEADS, what, :], head_rows[:, ft, :], sq[what][:, ft, :],
                                      start=ft == 0, stop=ft == KT - 1)
                    last.then_inc(norms_made, 1)
                pe.wait_ge(over_ready, b + 1)
                wait_alone(pe, norms_read, (b + 1) * NCH)
                mm(pb[0:1, 0, 0:1], over[:], ones[0:HEADS, 0:1], start=True, stop=True).then_inc(over_counted, 1)

            def score(n, par, u):
                c, j, off, _ = UNITS[u]
                pe.wait_ge(exped, n * NU + (u + 1))
                for h in range(2):
                    last = mm(scores[u % 2][:, h, off:], ks[par][0:QROWS, h, j * P:(j + 1) * P],
                              qs[par][0:QROWS, h, c * CH + off:(c + 1) * CH], start=True, stop=True)
                last.then_inc(scored, 1)

            def value(n, par, u):
                c, j, off, diag = UNITS[u]
                if u in FIRST:
                    pe.wait_ge(y_copied, n * NCH + (c + 1))
                if diag:
                    pe.wait_ge(masked, n * NDIAG + (DIAG[u] + 1))
                else:
                    pe.wait_ge(exped, n * NU + (u + 2 + 1))
                for h in range(2):
                    last = mm(pc[h * LAT:(h + 1) * LAT, c % 2, off:], vb[par][:, j, h * LAT:(h + 1) * LAT],
                              probs[u % NP_BUF][:, h, off:], start=u in FIRST, stop=u in LAST)
                last.then_inc(valued, 1)

            def denominators(n, g):
                last_unit = LAST[2 * g + 1]
                pe.wait_ge(summed, n * NU + (last_unit + NP_BUF + 1))
                pe.wait_ge(den_copied, n * GROUPS + (g + 1))
                for r in range(4):
                    last = mm(pd[32 * r:32 * (r + 1), g, :], ones[:], acc[2 * g + r // 2][:, r % 2, :],
                              start=True, stop=True)
                last.then_inc(den_made, 1)

            pe.wait_ge(wk_loaded, 32)
            pe.wait_ge(wc_loaded, 32)
            pe.wait_ge(ident_set, 1)
            pe.sem_inc(valued, NP_BUF)
            pe.sem_inc(den_made, GROUPS)
            for p in range(PAIRS):
                for ct in range(KT):
                    mm(pa[:, ct, p * 2 * HD:(p + 1) * 2 * HD], wk_raw[:, p, ct * P:(ct + 1) * P], wc_pair[:],
                       start=True, stop=True)
            per = P // (2 * HD)
            for p in range(PAIRS):
                r = p % per
                last = mm(pb[32 * r:32 * (r + 1), 0, p // per:p // per + 1], wc_pair[:], b_k_raw[:, p:p + 1],
                          start=True, stop=True)
            last.then_inc(kc_done, 1)
            pe.wait_ge(w_loaded, 16 * 11)
            pe.wait_ge(consts_set, 3)
            pe.wait_ge(kc_copied, 2)

            with pe.Fori(0, BATCH) as b:
                ffn(b, 0)
                projections(b)
                wait_alone(pe, flag_ready, b + 1)
                general = pe.value_load(flag[0:1, 0:1], min_val=0, max_val=HEADS)
                with pe.If(general > 0):
                    with pe.Fori(0, PAIRS) as p:
                        loads = len(PRODUCTS) * 32
                        wait_alone(pe, g_loaded, (b * PAIRS + p) * loads + loads)
                        for i in range(G_TURNS):
                            h, blk = divmod(i, NBLK)
                            pe.wait_ge(g_read, g_turn(b, p, i) + 1)
                            for k in range(blk // BPC + 1):
                                width = min(CH, (blk + 1) * P - k * CH)
                                last = mm(banks[k][:, 0:width], qs[0][0:QROWS - 1, h, blk * P:(blk + 1) * P],
                                          ks[0][0:QROWS - 1, h, k * CH:k * CH + width], start=True, stop=True)
                            last.then_inc(g_scored, 1)
                        wait_alone(pe, g_read, g_turn(b, p, G_TURNS) + 1)
                with pe.Else():
                    pe.sem_inc(g_scored, PAIRS * G_TURNS)
                wait_alone(pe, ones_rows, b * 2 + 2)
                with pe.Fori(0, PAIRS // 2) as pp:
                    n0 = b * PAIRS + pp * 2
                    for s in range(2 * NU + PV_LAG):
                        if s < 2 * NU:
                            par, u = divmod(s, NU)
                            if u == 0:
                                pe.wait_ge(pair_loaded[par], (b * (PAIRS // 2) + pp) * (16 * 14) + 16 * 14)
                            score(n0 + par, par, u)
                        v = s - PV_LAG
                        if v >= 0:
                            value(n0 + v // NU, v // NU, v % NU)
                        w = v - 2
                        if w >= 0 and w % NU in (LAST[1], LAST[3]) and w < 2 * NU:
                            denominators(n0 + w // NU, (LAST.index(w % NU)) // 2)
                    denominators(n0 + 1, GROUPS - 1)
                for half in range(2):
                    for p in range(PAIRS):
                        if half == 0:
                            pe.wait_ge(y_scaled, b * PAIRS + (p + 1) + 1)
                        for j in range(8):
                            blk = half * 8 + j
                            if p == 0 and half == 1:
                                pe.wait_ge(o_added, b * NBLK + (j + 1))
                            if p == 0 and half == 0 and j == 0:
                                pe.wait_ge(exped, (b + 1) * (PAIRS * NU) + 2)
                                pe.wait_ge(y_copied, (b + 1) * (PAIRS * NCH) + 2)
                                pe.wait_ge(den_copied, (b + 1) * (PAIRS * GROUPS) + 2)
                            last = mm(banks[j][:, 0:C], slots[:, p, blk * P:(blk + 1) * P], w_o[:, p, :],
                                      start=p == 0, stop=p == PAIRS - 1)
                            if p == PAIRS - 1:
                                last.then_inc(o_made, 1)
                ffn(b, 1)

        @block.scalar
        def _(act):
            A = nc.scalar.activation

            def copy_xnt(b, st, c):
                act.wait_ge(xnt_made, ln(b, st, c) + 1)
                if st != 1:
                    act.wait_ge(mixed, ff(b, st // 2, c) + 1)
                elif c < 2:
                    act.wait_ge(mixed, ff(b, 1, 0) + 1)
                else:
                    act.wait_ge(v_made, (b * NCH + (c - 1)) * VT)
                A(xnt[c % 2][:, :, 1:CH + 1], pa[:], ACT.Copy).then_inc(xnt_copied, 1)

            def ffn(b, w):
                copy_xnt(b, 2 * w, 0)
                for c in range(NCH):
                    act.wait_ge(gate_made, ff(b, w, c) + 1)
                    if c >= 2:
                        act.wait_ge(ffn_read, ff(b, w, c - 1) + 1)
                    A(gate[c % 2].rearrange("p (a b) c -> p a (b c)", a=2), pc[:], ACT.Sigmoid).then_inc(gate_ready, 1)
                    act.wait_ge(k_made, ff(b, w, c) + 1)
                    if c >= 2:
                        act.wait_ge(ffn_made, ff(b, w, c - 1))
                    A(kact[c % 2][:], pb[:], ACT.Relu).then_inc(k_relu, 1)
                    act.wait_ge(k_relu, ff(b, w, c) + 1 + 1)
                    A(kact[c % 2][:], kact[c % 2][:], ACT.Square).then_inc(kact_ready, 1)
                    if c + 1 < NCH:
                        copy_xnt(b, 2 * w, c + 1)

            for s in (xnt_copied, gate_ready, k_relu):
                act.sem_inc(s, 1)
            act.sem_inc(exped, 2)
            act.sem_inc(y_copied, 2)
            act.sem_inc(den_copied, 2)
            act.wait_ge(kc_done, 1)
            A(w_kc[:], pa[:, :, 0:C], ACT.Copy).then_inc(kc_copied, 1)
            A(b_kc[:], pb[:, 0, 0:KT], ACT.Copy).then_inc(kc_copied, 1)
            act.wait_ge(w_loaded, 16 * 11)
            act.wait_ge(kc_copied, 2)

            with act.Fori(0, BATCH) as b:
                ffn(b, 0)
                copy_xnt(b, 1, 0)
                for c in range(NCH):
                    turn = b * NCH + c
                    for what, (src, dst, bias, made, copied) in enumerate(((pb, qf, b_q, q_made, q_copied),
                                                                           (pc, kf, b_kc, kp_made, kp_copied))):
                        act.wait_ge(made, turn + 1)
                        if c > 0:
                            act.wait_ge((q_split, k_split)[what], turn)
                        for mt in range(KT):
                            last = A(dst[:, mt, :], src[:, mt, :], ACT.Identity, bias=bias[:, mt:mt + 1])
                        last.then_inc(copied, 1)
                    if c > 0:
                        act.wait_ge(norms_made, turn)
                    for what, (src, copied) in enumerate(((qf, q_copied), (kf, kp_copied))):
                        act.wait_ge(copied, turn + 1)
                        A(sq[what], src, ACT.Square).then_inc(squares, 1)
                    if c + 1 < NCH:
                        copy_xnt(b, 1, c + 1)
                act.wait_ge(bound_inputs, b + 1)
                A(qnorm, qnorm, ACT.Sqrt, scale=kmax[:, 0:1]).then_inc(bound_ready, 1)

                with act.Fori(0, PAIRS // 2) as pp:
                    n0 = b * PAIRS + pp * 2

                    def y_copy(v, c):
                        n, par = n0 + v // NU, v // NU
                        act.wait_ge(valued, n * NU + (LAST[c] + NP_BUF + 1))
                        dst = slots[:, bass.ds(pp * 2 + par, 1), c * CH:(c + 1) * CH].rearrange("p o n -> p (o n)")
                        A(dst, pc[:, c % 2, :], ACT.Copy).then_inc(y_copied, 1)

                    def den_copy(v, g):
                        n = n0 + v // NU
                        act.wait_ge(den_made, n * GROUPS + (g + GROUPS + 1))
                        act.wait_ge(den_sent, n * (16 * GROUPS) + 16)
                        A(den[:, g, :], pd[:, g, :], ACT.Copy).then_inc(den_copied, 1)

                    for s in range(2 * NU + 1):
                        if s < 2 * NU:
                            par, u = divmod(s, NU)
                            n, off = n0 + par, UNITS[u][2]
                            act.wait_ge(scored, n * NU + (u + 1))
                            act.wait_ge(valued, n * NU + (u + 1))
                            act.wait_ge(summed, n * NU + (u + 1))
                            A(probs[u % NP_BUF][:, :, off:], scores[u % 2][:, :, off:], ACT.Exp,
                              scale=SCALE).then_inc(exped, 1)
                        for v in range(2 * NU):
                            if v % NU in LAST and (s == v + 4 or s == 2 * NU and v + 4 >= 2 * NU):
                                y_copy(v, LAST.index(v % NU))
                        for v in range(2 * NU):
                            if v % NU in (LAST[1], LAST[3]) and (s == v + 8 or s == 2 * NU and v + 8 >= 2 * NU):
                                den_copy(v, LAST.index(v % NU) // 2)
                ffn(b, 1)

        @block.gpsimd
        def _(pool):
            g = nc.gpsimd
            g.memset(wc_pair[:], 0.0).then_inc(wc_zeroed, 1)
            pool.sem_inc(y_scaled, 1)
            g.memset(ident[:], 0.0).then_inc(pool_step, 1)
            g.memset(ones[:], 1.0).then_inc(consts_set, 1)
            g.memset(eps_half[:], -0.5).then_inc(pool_step, 1)
            g.memset(head_rows[:], 1.0).then_inc(pool_step, 1)
            g.memset(tri[:], 0.0).then_inc(pool_step, 1)
            pool.wait_ge(pool_step, 4)
            g.affine_select(out=ident[:], in_=ident[:], compare_op=ALU.not_equal, fill=1.0, base=0,
                            pattern=[[-1, P]], channel_multiplier=1).then_inc(ident_set, 1)
            g.affine_select(out=tri[:], in_=tri[:], compare_op=ALU.is_ge, fill=MASKED, base=0,
                            pattern=[[-1, P]], channel_multiplier=1).then_inc(consts_set, 1)
            hr = head_rows[:]
            g.affine_select(out=hr, in_=hr, compare_op=ALU.is_ge, fill=0.0, base=0,
                            pattern=[[P, KT], [-HD, HEADS]], channel_multiplier=1).then_inc(pool_step, 1)
            pool.wait_ge(pool_step, 5)
            g.affine_select(out=hr, in_=hr, compare_op=ALU.is_ge, fill=0.0, base=HD - 1,
                            pattern=[[-P, KT], [HD, HEADS]], channel_multiplier=-1).then_inc(consts_set, 1)

            def ln_power(b, st, c):
                turn = ln(b, st, c)
                wait_alone(pool, stats_ready, turn + 1)
                g.tensor_scalar(rstd[:, c % 2, :], mv[:, c % 2, :, 1], EPS, None, ALU.add).then_inc(pool_step, 1)
                pool.wait_ge(pool_step, turn + 6)
                g.tensor_tensor(rstd[:, c % 2, :], rstd[:, c % 2, :], eps_half[:], ALU.pow).then_inc(rstd_ready, 1)

            with pool.Fori(0, BATCH) as b:
                for st in range(2):
                    for c in range(NCH):
                        ln_power(b, st, c)
                pool.wait_ge(xn_ready, ln(b, 1, NCH - 1) + 1)
                pool.wait_ge(w_loaded, 16 * 11)
                for i in range(NBLK):
                    g.tensor_tensor(x_sb[:, i, :], x_sb[:, i, :], b_o[:], ALU.add).then_inc(bo_added, 1)

                def scale_y(n, p):
                    pool.wait_ge(rden_back, n * 32 + 32)
                    pool.wait_ge(y_copied, n * NCH + (NCH + 2))
                    y = slots[:, bass.ds(p, 1), :].rearrange("p o n -> p (o n)")
                    g.tensor_tensor(y, y, rden[:].rearrange("p a b -> p (a b)"), ALU.mult).then_inc(y_scaled, 1)

                with pool.Fori(0, PAIRS // 2) as pp:
                    n0 = b * PAIRS + pp * 2
                    for par in range(2):
                        for u, (c, j, off, diag) in enumerate(UNITS):
                            if diag:
                                wait_alone(pool, exped, (n0 + par) * NU + (u + 3))
                                tile = probs[u % NP_BUF][:, :, off:off + P]
                                g.affine_select(out=tile, in_=tile, compare_op=ALU.is_ge, fill=0.0, base=0,
                                                pattern=[[0, 2], [1, P]], channel_multiplier=-1).then_inc(masked, 1)
                            if u == LAST[2]:
                                if par == 0:
                                    with pool.If(pp > 0):
                                        before = nc.s_assert_within(
                                            pp * 2 - 1, 0, PAIRS - 1,
                                            skip_runtime_bounds_check_because="the first turn is left out")
                                        scale_y(n0 - 1, before)
                                else:
                                    scale_y(n0, pp * 2)
                scale_y(b * PAIRS + (PAIRS - 1), PAIRS - 1)
                for c in range(NCH):
                    ln_power(b, 2, c)

        @block.vector
        def _(dve):
            v = nc.vector
            count = [0]

            def link(b, ins, alone=False):
                count[0] += 1
                ins.then_inc(dve_step, 1)
                (wait_alone if alone else type(dve).wait_ge)(dve, dve_step, b * STEPS + count[0])

            def ln_stats(b, st, c):
                if st == 0:
                    dve.wait_ge(x_loaded[c], b * 16 + 16)
                elif st == 1:
                    dve.wait_ge(ffn_added, ff(b, 0, c) + 1)
                else:
                    dve.wait_ge(o_added, b * NBLK + (c + 1) * BPC)
                for i in range(BPC):
                    last = v.bn_stats(stats[:, c % 2, i, :], x_sb[:, c * BPC + i, :])
                link(b, last, alone=True)
                for i in range(BPC):
                    last = v.bn_aggr(mv[:, c % 2, i, :], stats[:, c % 2, i, :])
                last.then_inc(stats_ready, 1)

            def ln_apply(b, st, c):
                turn = ln(b, st, c)
                dve.wait_ge(rstd_ready, turn + 1)
                if c >= 2:
                    dve.wait_ge(xnt_made, turn - 1)
                elif st > 0:
                    dve.wait_ge(xnt_made, ln(b, st, 0))
                for i in range(BPC):
                    last = v.tensor_scalar(xn[c % 2][:, i, :], x_sb[:, c * BPC + i, :], mv[:, c % 2, i, 0:1],
                                           rstd[:, c % 2, i:i + 1], ALU.subtract, ALU.mult)
                last.then_inc(xn_ready, 1)

            def mix(b, w, c):
                cur, old = xnt[c % 2], xnt[(c + 1) % 2]
                dve.wait_ge(xnt_copied, ln(b, 2 * w, c) + 1 + 1)
                if c == 0:
                    link(b, v.memset(cur[:, :, 0:1], 0.0))
                else:
                    link(b, v.tensor_copy(cur[:, :, 0:1], old[:, :, CH:CH + 1]))
                if c >= 2:
                    dve.wait_ge(k_made, ff(b, w, c - 1))
                link(b, v.tensor_tensor(diff, cur[:, :, 1:CH + 1], cur[:, :, 0:CH], ALU.subtract))
                for dst, mu in ((x_r, mur), (x_k, muk)):
                    for kt in range(KT):
                        last = v.scalar_tensor_tensor(dst[c % 2][:, kt, :], diff[:, kt, :], mu[:, kt:kt + 1],
                                                      cur[:, kt, 0:CH], ALU.mult, ALU.add)
                last.then_inc(mixed, 1)

            def add_ffn(b, w, c):
                dve.wait_ge(ffn_made, ff(b, w, c) + 1)
                dve.wait_ge(gate_ready, ff(b, w, c) + 1 + 1)
                v.scalar_tensor_tensor(prod, pd[:].rearrange("p a (b c) -> p (a b) c", c=C), 0.5,
                                       gate[c % 2], ALU.mult, ALU.mult).then_inc(ffn_read, 1)
                dve.wait_ge(ffn_read, ff(b, w, c) + 1 + 1)
                xc = x_sb[:, c * BPC:(c + 1) * BPC, :]
                ins = v.tensor_tensor(xc, xc, prod, ALU.add)
                ins.then_inc(ffn_added, 1)

            def ffn(b, w):
                st = 2 * w
                ln_stats(b, st, 0)
                ln_apply(b, st, 0)
                for c in range(NCH):
                    if c + 1 < NCH:
                        ln_stats(b, st, c + 1)
                    mix(b, w, c)
                    if c + 1 < NCH:
                        ln_apply(b, st, c + 1)
                    add_ffn(b, w, c)

            dve.wait_ge(w_loaded, 16 * 11)
            dve.wait_ge(consts_set, 3)
            dve.sem_inc(summed, NP_BUF)
            for s in (ffn_read, mixed, g_read):
                dve.sem_inc(s, 1)
            with dve.Fori(0, BATCH) as b:
                ffn(b, 0)
                ln_stats(b, 1, 0)
                ln_apply(b, 1, 0)
                for c in range(NCH):
                    turn = b * NCH + c
                    if c + 1 < NCH:
                        ln_stats(b, 1, c + 1)
                        ln_apply(b, 1, c + 1)

                    def store_v(i):
                        blk, half = c * BPC + i // 2, i % 2
                        dve.wait_ge(v_made, turn * VT + (i + 1))
                        per = PAIRS // 2
                        dst = slots[:, half * per:(half + 1) * per, blk * P:(blk + 1) * P]
                        v.tensor_tensor(dst, pd[:, i % 2, :].rearrange("p (a b) -> p a b", a=per),
                                        b_val[:, half * CH:(half + 1) * CH].rearrange("p (a b) -> p a b", a=per),
                                        ALU.add).then_inc(v_stored, 1)

                    for what, (src, parts, copied, saved, split) in enumerate((
                            (qf, q_parts, q_copied, q_saved, q_split), (kf, k_parts, kp_copied, k_saved, k_split))):
                        store_v(4 * what)
                        dve.wait_ge(copied, turn + 1)
                        dve.wait_ge(saved, turn * 16 + 16)
                        link(b, v.tensor_copy(parts[:, 0], src))
                        store_v(4 * what + 1)
                        link(b, v.tensor_tensor(rest[what][:], src, parts[:, 0], ALU.subtract))
                        store_v(4 * what + 2)
                        link(b, v.tensor_copy(parts[:, 1], rest[what][:]))
                        store_v(4 * what + 3)
                        v.tensor_tensor(parts[:, 2], rest[what][:], parts[:, 1], ALU.subtract).then_inc(split, 1)
                    dve.wait_ge(norms_made, turn + 1)
                    v.tensor_copy(qnorm[:, c * CH:(c + 1) * CH], pb[0:HEADS, 0, :])
                    v.tensor_reduce(kmax4[:, c:c + 1], pb[0:HEADS, 1, :], AX.X, ALU.max).then_inc(norms_read, 1)
                dve.wait_ge(norms_read, (b + 1) * NCH)
                v.tensor_reduce(kmax[:], kmax4[:], AX.X, ALU.max).then_inc(bound_inputs, 1)
                dve.wait_ge(bound_ready, b + 1)
                v.tensor_scalar(shift, qnorm, -MARGIN, None, ALU.mult).then_inc(shift_ready, 1)
                link(b, v.tensor_reduce(kmax4[:, 0:1], qnorm, AX.X, ALU.max))
                v.tensor_scalar(over[:], kmax4[:, 0:1], SAFE, None, ALU.is_gt).then_inc(over_ready, 1)
                dve.wait_ge(over_counted, b + 1)
                v.tensor_copy(flag[:], pb[0:1, 0, 0:1]).then_inc(flag_ready, 1)

                dve.wait_ge(k_saved, b * (16 * NCH) + 16 * NCH + 16)
                dve.wait_ge(q_saved, b * (16 * NCH) + 16 * NCH + 16)
                for i in range(2):
                    v.memset(ks[i][QROWS - 1:QROWS, :, :], 1.0).then_inc(ones_rows, 1)

                wait_alone(dve, flag_ready, b + 1)
                general = dve.value_load(flag[0:1, 0:1], min_val=0, max_val=HEADS)
                with dve.If(general > 0):
                    with dve.Fori(0, PAIRS) as p:
                        wait_alone(dve, g_sent, (b * PAIRS + p) * 16 + 16)
                        for i in range(G_TURNS):
                            h, blk = divmod(i, NBLK)
                            k, low = blk // BPC, blk % BPC * P
                            turn = g_turn(b, p, i)

                            def g_link(ins, step):
                                ins.then_inc(g_step, 1)
                                dve.wait_ge(g_step, turn * G_STEPS + step)

                            g_link(v.memset(g_part[:], MASKED), 1)
                            dve.wait_ge(g_scored, turn + 1)
                            for full in range(k):
                                v.tensor_reduce(g_part[:, full:full + 1], banks[full][:], AX.X, ALU.max)
                            if low:
                                v.tensor_reduce(g_part[:, k:k + 1], banks[k][:, 0:low], AX.X, ALU.max)
                            g_link(v.tensor_tensor(g_diag, banks[k][:, low:low + P], tri[:], ALU.add), 2)
                            g_link(v.tensor_reduce(g_part[:, NCH:NCH + 1], g_diag, AX.X, ALU.max), 3)
                            g_link(v.tensor_reduce(g_top[:], g_part[:], AX.X, ALU.max), 4)
                            last = v.tensor_scalar(g_shift[:, h, blk:blk + 1], g_top[:], -1.0, None, ALU.mult)
                            last.then_inc(g_read, 1)
                        dve.wait_ge(g_read, g_turn(b, p, G_TURNS) + 1)
                        dve.sem_inc(g_max, 1)
                with dve.Else():
                    dve.sem_inc(g_step, PAIRS * G_TURNS * G_STEPS)
                    dve.sem_inc(g_read, PAIRS * G_TURNS)
                    dve.sem_inc(g_max, PAIRS)

                def invert(n):
                    dve.wait_ge(den_back, n * 16 + 16)
                    v.reciprocal(rden_c[:], den_c[:]).then_inc(rden_made, 1)

                with dve.Fori(0, PAIRS // 2) as pp:
                    n0 = b * PAIRS + pp * 2
                    for par in range(2):
                        n = n0 + par
                        for u, (c, j, off, diag) in enumerate(UNITS):
                            if diag:
                                dve.wait_ge(masked, n * NDIAG + (DIAG[u] + 1))
                            else:
                                dve.wait_ge(exped, n * NU + (u + 3))
                            if u in FIRST:
                                dve.wait_ge(den_made, n * GROUPS + (c // 2 + 1))
                                v.tensor_copy(acc[c][:], probs[u % NP_BUF][:]).then_inc(summed, 1)
                            else:
                                dve.wait_ge(summed, n * NU + (u + NP_BUF))
                                a = acc[c][:, :, off:]
                                v.tensor_tensor(a, a, probs[u % NP_BUF][:, :, off:], ALU.add).then_inc(summed, 1)
                            if u == 16:
                                if par == 0:
                                    with dve.If(pp > 0):
                                        invert(n0 - 1)
                                else:
                                    invert(n0)
                invert(b * PAIRS + (PAIRS - 1))
                dve.wait_ge(bo_added, (b + 1) * NBLK)
                for blk in range(NBLK):
                    dve.wait_ge(o_made, b * NBLK + (blk + 1))
                    v.tensor_tensor(x_sb[:, blk, :], x_sb[:, blk, :], banks[blk % 8][:, 0:C],
                                    ALU.add).then_inc(o_added, 1)
                ffn(b, 1)
            assert count[0] == STEPS, count[0]


STEPS = 53
_IN = ["x", "ffn_wr", "ffn_wk", "ffn_wv", "mu_r", "mu_k", "wq", "bq", "wk_t", "bk", "wc_t", "wv", "bv", "wo", "bo"]


def _layout(inputs):
    import numpy as np
    a = {k.removeprefix("L0_"): np.asarray(v) for k, v in inputs.items()}

    def rows(w, n=128):
        return np.ascontiguousarray(w.reshape(-1, n, w.shape[-1]).transpose(1, 0, 2))

    def cols(v, n=128):
        return np.ascontiguousarray(v.reshape(-1, n).T)

    return {
        "x": a["attn_x"].reshape(-1, a["attn_x"].shape[-1]),
        "ffn_wr": rows(a["ffn_W_r"].T), "ffn_wk": rows(a["ffn_W_k"].T), "ffn_wv": rows(a["ffn_W_v"].T),
        "mu_r": cols(a["ffn_mu_r"]), "mu_k": cols(a["ffn_mu_k"]),
        "wq": rows(a["attn_Wq"]), "bq": cols(a["attn_bq"]),
        "wk_t": rows(a["attn_Wk"].T), "bk": cols(a["attn_bk"]), "wc_t": np.ascontiguousarray(a["attn_Wc"].T),
        "wv": rows(a["attn_Wv"]), "bv": a["attn_bv"].reshape(1, -1), "wo": rows(a["attn_Wo"]),
        "bo": a["attn_bo"].reshape(1, -1),
    }


def kernel(**inputs):
    import numpy as np
    import concourse.bacc as bacc
    from concourse.bass_utils import run_bass_kernel_spmd

    batch, t, c = inputs["L0_attn_x"].shape
    heads = 16
    arrays = {f"in_{k}": v for k, v in _layout(inputs).items()}
    nc = bacc.Bacc("TRN2", target_bir_lowering=False, num_devices=1)
    ins = [nc.dram_tensor(f"in_{k}", arrays[f"in_{k}"].shape, mybir.dt.from_np(arrays[f"in_{k}"].dtype),
                          kind="ExternalInput").ap() for k in _IN]
    out = nc.dram_tensor("out", (batch * t, c), mybir.dt.float32, kind="ExternalOutput").ap()
    qk = nc.dram_tensor("qk_scratch", (batch, 2, 3, c, t), mybir.dt.bfloat16, kind="Internal").ap()
    shift = nc.dram_tensor("shift_scratch", (batch, heads, t), mybir.dt.bfloat16, kind="Internal").ap()
    den = nc.dram_tensor("den_scratch", (2, 4, 512), mybir.dt.float32, kind="Internal").ap()
    rden = nc.dram_tensor("rden_scratch", (2, 4, 512), mybir.dt.float32, kind="Internal").ap()
    macaron_block(nc, ins[0], out, *ins[1:], qk, shift, den, rden)
    r = run_bass_kernel_spmd(nc, [arrays], core_ids=[0])
    return np.asarray(r.results[0]["out"]).reshape(batch, t, c)
```

```python
import concourse.bass as bass
from concourse import mybir
from contextlib import ExitStack


def macaron_block(nc, x, out, ffn_wr, ffn_wk, ffn_wv, mu_r, mu_k, wq, bq, wk_t, bk, wc_t, wv, bv, wo, bo,
                  qk_scratch, shift_scratch, den_scratch, rden_scratch):
    fp32, bf16, i32 = mybir.dt.float32, mybir.dt.bfloat16, mybir.dt.int32
    ALU, ACT, AX = mybir.AluOpType, mybir.ActivationFunctionType, mybir.AxisListType

    P = 128
    C = wq.shape[2]
    BATCH = qk_scratch.shape[0]
    T = x.shape[0] // BATCH
    KT = C // P
    CH = 512
    NCH = T // CH
    BPC = CH // P
    NBLK = T // P
    HEADS, LAT = 16, 64
    HD = C // HEADS
    PAIRS = HEADS // 2
    PRODUCTS = ((0, 0), (0, 1), (0, 2), (1, 0), (1, 1), (2, 0))
    QROWS = len(PRODUCTS) * HD + 1
    SCALE = LAT ** -0.5
    EPS = 1e-5
    SAFE = 35.0 / SCALE
    MARGIN = 1.01
    MASKED = -3.0e38

    UNITS = []
    for c in range(NCH):
        UNITS += [(c, j, 0, False) for j in range(BPC * c)]
        UNITS += [(c, BPC * c + i, P * i, True) for i in range(BPC)]
    NU = len(UNITS)
    FIRST = [u for u in range(NU) if u == 0 or UNITS[u - 1][0] != UNITS[u][0]]
    LAST = [u for u in range(NU) if u == NU - 1 or UNITS[u + 1][0] != UNITS[u][0]]
    DIAG = [sum(UNITS[v][3] for v in range(u)) for u in range(NU)]
    NDIAG = NCH * BPC
    NP_BUF = 4
    PV_LAG = 3
    GROUPS = NCH // 2
    assert NU % NP_BUF == 0 and NU % 2 == 0

    ctx = ExitStack()
    with ctx:
        def sb(name, shape, dt=fp32):
            return ctx.enter_context(nc.sbuf_tensor(name, shape, dt))

        def sem(name):
            return ctx.enter_context(nc.semaphore(name))

        w_r, w_k, w_v = sb("w_r", [P, KT, C]), sb("w_k", [P, KT, C]), sb("w_v", [P, KT, C])
        mur, muk = sb("mur", [P, KT]), sb("muk", [P, KT])
        w_q, b_q = sb("w_q", [P, KT, C]), sb("b_q", [P, KT])
        w_kc, b_kc = sb("w_kc", [P, KT, C]), sb("b_kc", [P, KT])
        w_val, b_val = sb("w_val", [P, KT, HEADS * LAT]), sb("b_val", [P, HEADS * LAT])
        w_o, b_o = sb("w_o", [P, PAIRS, C]), sb("b_o", [P, C])
        b_k_raw = sb("b_k_raw", [P, PAIRS])
        wc_pair = sb("wc_pair", [P, 2 * HD])
        ident = sb("ident", [P, P])
        ones = sb("ones", [P, 32])
        head_rows = sb("head_rows", [P, KT, HEADS], bf16)
        eps_half = sb("eps_half", [P, BPC])
        tri = sb("tri", [P, P])

        x_sb = sb("x_sb", [P, NBLK, C])
        slots = sb("slots", [P, PAIRS, NBLK * P])
        stats = sb("stats", [P, 2, BPC, 6])
        mv = sb("mv", [P, 2, BPC, 2])
        rstd = sb("rstd", [P, 2, BPC])
        kmax4, kmax, over = sb("kmax4", [HEADS, NCH]), sb("kmax", [HEADS, 1]), sb("over", [HEADS, 1])
        flag = sb("flag", [1, 1], i32)

        qs = [sb(f"qs{i}", [P, 2, T], bf16) for i in range(2)]
        ks = [sb(f"ks{i}", [P, 2, T], bf16) for i in range(2)]
        vb = [sb(f"vb{i}", [P, NBLK, P]) for i in range(2)]
        probs = [sb(f"probs{i}", [P, 2, CH]) for i in range(NP_BUF)]
        acc = [sb(f"acc{i}", [P, 2, CH]) for i in range(NCH)]
        den = sb("den", [P, GROUPS, CH])
        den_c, rden_c = sb("den_c", [P, 2 * T // P]), sb("rden_c", [P, 2 * T // P])
        rden = sb("rden", [P, NCH, CH])

        def view(t, k, n, shape):
            flat = t[:].rearrange("p a b -> p (a b)")[:, 2 * k:2 * (k + n)].bitcast(fp32)
            return flat.rearrange("p (a b) -> p a b", a=shape[0])
        W = CH * KT
        xn = [view(qs[0], i * W, W, (BPC, C)) for i in range(2)]
        x_r = [view(qs[1], i * W, W, (KT, CH)) for i in range(2)]
        x_k = [view(ks[0], i * W, W, (KT, CH)) for i in range(2)]
        diff = view(ks[1], 0, W, (KT, CH))
        prod = view(ks[1], W, W, (BPC, C))
        kact = [probs[i] for i in range(2)]
        gate = [probs[2 + i][:].rearrange("p a (b c) -> p (a b) c", b=BPC // KT) for i in range(2)]
        xnt = [vb[i][:].rearrange("p a b -> p (a b)")[:, 0:KT * (CH + 2)].rearrange("p (a b) -> p a b", a=KT)
               for i in range(2)]
        xt = [t[:] for t in acc]
        qf, kf = view(qs[1], 0, W, (KT, CH)), view(qs[1], W, W, (KT, CH))
        q_parts = ks[0][:].rearrange("p a b -> p (a b)")[:, 0:3 * W].rearrange("p (s a b) -> p s a b", s=3, a=KT)
        k_parts = ks[1][:].rearrange("p a b -> p (a b)")[:, 0:3 * W].rearrange("p (s a b) -> p s a b", s=3, a=KT)
        rest = [probs[0], probs[1]]
        sq = [probs[2 + i][:].rearrange("p a b -> p (a b)")[:, 0:W // 2].bitcast(bf16)
              .rearrange("p (a b) -> p a b", a=KT) for i in range(2)]
        qnorm = rden[0:HEADS].rearrange("p a b -> p (a b)")
        shift = den[0:HEADS].rearrange("p a b -> p (a b)").bitcast(bf16)
        wk_raw = slots[:].rearrange("p a b -> p (a b)")[:, 0:PAIRS * C].rearrange("p (a b) -> p a b", a=PAIRS)

        pa, pb, pc, pd = (ctx.enter_context(nc.psum_tensor(n, [P, 2, CH], fp32)) for n in ("pa", "pb", "pc", "pd"))
        scores = [pa, pb]
        banks = [t[:, i, :] for t in (pa, pb, pc, pd) for i in range(2)]

        w_loaded, wc_zeroed, wc_loaded, wk_loaded = sem("w_loaded"), sem("wc_zeroed"), sem("wc_loaded"), sem("wk_loaded")
        attn_w_loaded = sem("attn_w_loaded")
        consts_set, ident_set, kc_done, kc_copied = sem("consts_set"), sem("ident_set"), sem("kc_done"), sem("kc_copied")
        x_loaded = [sem(f"x_loaded{c}") for c in range(NCH)]
        out_stored = [sem(f"out_stored{c}") for c in range(NCH)]
        dve_step, waited = sem("dve_step"), sem("waited")
        stats_ready, rstd_ready, xn_ready = sem("stats_ready"), sem("rstd_ready"), sem("xn_ready")
        pool_step = sem("pool_step")
        xnt_made, xnt_copied = sem("xnt_made"), sem("xnt_copied")
        mixed = sem("mixed")
        gate_made, gate_ready = sem("gate_made"), sem("gate_ready")
        k_made, k_relu, kact_ready = sem("k_made"), sem("k_relu"), sem("kact_ready")
        ffn_made, ffn_read, ffn_added = sem("ffn_made"), sem("ffn_read"), sem("ffn_added")
        q_made, kp_made, v_made = sem("q_made"), sem("kp_made"), sem("v_made")
        q_copied, kp_copied, squares = sem("q_copied"), sem("kp_copied"), sem("squares")
        rounded = sem("rounded")
        v_stored, q_split, k_split = sem("v_stored"), sem("q_split"), sem("k_split")
        q_saved, k_saved = sem("q_saved"), sem("k_saved")
        norms_made, norms_read = sem("norms_made"), sem("norms_read")
        bound_inputs, bound_ready, shift_ready, shift_saved = (
            sem("bound_inputs"), sem("bound_ready"), sem("shift_ready"), sem("shift_saved"))
        over_ready, over_counted, flag_ready = sem("over_ready"), sem("over_counted"), sem("flag_ready")
        pair_loaded = [sem(f"pair_loaded{i}") for i in range(2)]
        ones_rows = sem("ones_rows")
        scored, exped, masked, summed, valued = sem("scored"), sem("exped"), sem("masked"), sem("summed"), sem("valued")
        y_copied, den_made, den_copied = sem("y_copied"), sem("den_made"), sem("den_copied")
        den_sent, den_back, rden_made, rden_sent, rden_back = (
            sem("den_sent"), sem("den_back"), sem("rden_made"), sem("rden_sent"), sem("rden_back"))
        y_scaled, bo_added, o_made, o_added = sem("y_scaled"), sem("bo_added"), sem("o_made"), sem("o_added")
        g_loaded, g_scored, g_read, g_max, g_sent, g_step = (
            sem("g_loaded"), sem("g_scored"), sem("g_read"), sem("g_max"), sem("g_sent"), sem("g_step"))

        LN_TURNS, FFN_TURNS = 3 * NCH, 2 * NCH
        V_TILES = NBLK * HEADS * LAT // CH

        def ln(b, st, c):
            return b * LN_TURNS + (st * NCH + c)

        def ff(b, w, c):
            return b * FFN_TURNS + (w * NCH + c)

        def the_pair_before(pp):
            return nc.s_assert_within(pp * 2 - 1, 0, PAIRS - 1,
                                      skip_runtime_bounds_check_because="the first turn is left out")

        def wait_alone(eng, s, count):
            eng.wait_ge(s, count)
            eng.sem_inc(waited, 1)

        G_TURNS, G_STEPS = 2 * NBLK, 4
        g_part = sb("g_part", [P, NCH + 1])
        g_diag = probs[0][:, 0, 0:P]
        g_top = sb("g_top", [P, 1])
        g_shift = sb("g_shift", [P, 2, NBLK], bf16)

        def g_turn(b, p, i):
            return (b * PAIRS + p) * G_TURNS + i

        O_BANKS = 6
        LOADS = 16 * (2 * len(PRODUCTS) + 2)

        block = ctx.enter_context(nc.Block())

        @block.sync
        def _(sp):
            for s, n in ((q_saved, 16), (k_saved, 16), (g_sent, 16), (den_sent, 48)):
                sp.sem_inc(s, n)
            def load_x0(c):
                rows = x[c * CH:(c + 1) * CH, :].rearrange("(n p) c -> p n c", p=P)
                sp.dma_start(x_sb[:, c * BPC:(c + 1) * BPC, :], rows).then_inc(x_loaded[c], 16)

            load_x0(0)
            sp.dma_start(wk_raw, wk_t).then_inc(wk_loaded, 16)
            sp.dma_start(b_k_raw[:], bk).then_inc(wk_loaded, 16)
            sp.wait_ge(wc_zeroed, 1)
            for i in range(2):
                sp.dma_start(wc_pair[i * LAT:(i + 1) * LAT, i * HD:(i + 1) * HD], wc_t).then_inc(wc_loaded, 16)
            load_x0(1)
            for dst, src in ((mur, mu_r), (muk, mu_k), (w_k, ffn_wk), (w_r, ffn_wr), (w_v, ffn_wv)):
                sp.dma_start(dst[:], src).then_inc(w_loaded, 16)
            for c in range(2, NCH):
                load_x0(c)
            for dst, src in ((w_q, wq), (b_q, bq), (w_val, wv), (w_o, wo)):
                sp.dma_start(dst[:], src).then_inc(attn_w_loaded, 16)
            sp.dma_start(b_val[:], bv.to_broadcast([P, HEADS * LAT])).then_inc(attn_w_loaded, 16)
            sp.dma_start(b_o[:], bo.to_broadcast([P, C])).then_inc(attn_w_loaded, 16)

            def part_rows(b, p, what, part):
                src = qk_scratch[b, what, part, bass.ds(p * (2 * HD), 2 * HD), :]
                return src.rearrange("(h d) t -> d h t", h=2)

            def load_pair(b, p, par):
                for s, (qp, kp) in enumerate(PRODUCTS):
                    rows = slice(s * HD, (s + 1) * HD)
                    sp.dma_start(qs[par][rows, :, :], part_rows(b, p, 0, qp)).then_inc(pair_loaded[par], 16)
                    sp.dma_start(ks[par][rows, :, :], part_rows(b, p, 1, kp)).then_inc(pair_loaded[par], 16)
                src = shift_scratch[b, bass.ds(p * 2, 2), :].rearrange("(o h) t -> o h t", o=1)
                sp.dma_start(qs[par][QROWS - 1:QROWS, :, :], src).then_inc(pair_loaded[par], 16)
                sp.dma_start(vb[par][:].rearrange("p a b -> p (a b)"),
                             slots[:, bass.ds(p, 1), :].rearrange("p o n -> p (o n)")).then_inc(pair_loaded[par], 16)

            def reciprocals(n):
                for g in range(GROUPS):
                    sp.wait_ge(den_copied, n * GROUPS + (2 + g + 1))
                    sp.dma_start(den_scratch[g], den[0:P:32, g, :]).then_inc(den_sent, 16)
                sp.wait_ge(den_sent, n * (16 * GROUPS) + (16 * GROUPS + 48))
                sp.dma_start(den_c[:], den_scratch.rearrange("g r (a c) -> (g r a) c", c=2 * T // P)).then_inc(den_back, 16)
                sp.wait_ge(rden_made, n + 1)
                sp.dma_start(rden_scratch.rearrange("g r (a c) -> (g r a) c", c=2 * T // P), rden_c[:]).then_inc(rden_sent, 16)
                sp.wait_ge(rden_sent, n * 16 + 16)
                sp.wait_ge(y_scaled, n + 1)
                for h in range(2):
                    src = rden_scratch.rearrange("g (c h) n -> h (g c) n", h=2)[h:h + 1]
                    sp.dma_start(rden[h * LAT:(h + 1) * LAT, :, :],
                                 src.to_broadcast([LAT, NCH, CH])).then_inc(rden_back, 16)

            def load_x(row, c):
                rows = x[bass.ds(row * T + c * CH, CH), :].rearrange("(n p) c -> p n c", p=P)
                sp.dma_start(x_sb[:, c * BPC:(c + 1) * BPC, :], rows).then_inc(x_loaded[c], 16)

            with sp.Fori(0, BATCH) as b:
                for c in range(NCH):
                    for what, parts, split, saved in ((0, q_parts, q_split, q_saved), (1, k_parts, k_split, k_saved)):
                        sp.wait_ge(split, b * NCH + (c + 1))
                        dst = qk_scratch[b, what, :, :, c * CH:(c + 1) * CH].rearrange("s (f p) t -> p (s f) t", p=P)
                        sp.dma_start(dst, parts.rearrange("p s f t -> p (s f) t")).then_inc(saved, 16)
                sp.wait_ge(shift_ready, b + 1)
                sp.dma_start(shift_scratch[b], shift).then_inc(shift_saved, 16)
                wait_alone(sp, q_saved, b * (16 * NCH) + 16 * NCH + 16)
                wait_alone(sp, k_saved, b * (16 * NCH) + 16 * NCH + 16)
                wait_alone(sp, shift_saved, b * 16 + 16)
                wait_alone(sp, xnt_made, ln(b, 2, 0))
                wait_alone(sp, flag_ready, b + 1)
                general = sp.value_load(flag[0:1, 0:1], min_val=0, max_val=HEADS)
                with sp.If(general > 0):
                    with sp.Fori(0, PAIRS) as p:
                        for s, (qp, kp) in enumerate(PRODUCTS):
                            rows = slice(s * HD, (s + 1) * HD)
                            sp.dma_start(qs[0][rows, :, :], part_rows(b, p, 0, qp)).then_inc(g_loaded, 16)
                            sp.dma_start(ks[0][rows, :, :], part_rows(b, p, 1, kp)).then_inc(g_loaded, 16)
                        sp.wait_ge(g_max, b * PAIRS + p + 1)
                        dst = shift_scratch[b, bass.ds(p * 2, 2), :].rearrange("h (n p) -> p h n", p=P)
                        with nc.allow_non_contiguous_dma(reason="a column of maxima becomes a row"):
                            sp.dma_start(dst, g_shift[:]).then_inc(g_sent, 16)
                        wait_alone(sp, g_sent, (b * PAIRS + p) * 16 + 32)
                with sp.Else():
                    sp.sem_inc(g_loaded, PAIRS * len(PRODUCTS) * 32)
                    sp.sem_inc(g_sent, PAIRS * 16)
                wait_alone(sp, v_stored, b * V_TILES + V_TILES // 2)
                for par in range(2):
                    load_pair(b, par, par)
                wait_alone(sp, v_stored, b * V_TILES + V_TILES)
                with sp.Fori(0, PAIRS // 2) as pp:
                    for par in range(2):
                        n = b * PAIRS + pp * 2 + par
                        wait_alone(sp, valued, n * NU + (NU + NP_BUF))
                        with sp.If(pp < PAIRS // 2 - 1):
                            later = nc.s_assert_within(pp * 2 + (par + 2), 0, PAIRS - 1,
                                                       skip_runtime_bounds_check_because="the last turn is left out")
                            load_pair(b, later, par)
                        reciprocals(n)
                for c in range(NCH):
                    sp.wait_ge(ffn_added, ff(b, 1, c) + 1)
                    rows = out[bass.ds(b * T + c * CH, CH), :].rearrange("(n p) c -> p n c", p=P)
                    sp.dma_start(rows, x_sb[:, c * BPC:(c + 1) * BPC, :]).then_inc(out_stored[c], 16)
                    wait_alone(sp, out_stored[c], b * 16 + 16)
                    with sp.If(b < BATCH - 1):
                        row = nc.s_assert_within(b + 1, 0, BATCH - 1,
                                                 skip_runtime_bounds_check_because="the last row is left out")
                        load_x(row, c)
            sp.wait_ge(rden_back, 32 * PAIRS * BATCH)

        @block.tensor
        def _(pe):
            mm = nc.tensor.matmul

            def transposes(b, st, c):
                pe.wait_ge(xn_ready, ln(b, st, c) + 1)
                pe.wait_ge(xnt_copied, ln(b, st, c) + 1)
                for ft in range(KT):
                    for i in range(BPC):
                        last = nc.tensor.transpose(pa[:, ft, i * P:(i + 1) * P], xn[c % 2][:, i, ft * P:(ft + 1) * P],
                                                   ident[:])
                last.then_inc(xnt_made, 1)

            def ffn(b, w):
                for c in range(NCH):
                    if w == 1 and c == NCH - 1:
                        with pe.If(b < BATCH - 1):
                            transposes(b + 1, 0, 0)
                    pe.wait_ge(mixed, ff(b, w, c) + 1 + 1)
                    pe.wait_ge(k_relu, ff(b, w, c) + 1)
                    if w == 1 and c == 0:
                        pe.wait_ge(o_added, b * NBLK + NBLK)
                    for mt in range(KT):
                        for kt in range(KT):
                            last = mm(pb[:, mt, :], w_k[:, kt, mt * P:(mt + 1) * P], x_k[c % 2][:, kt, :],
                                      start=kt == 0, stop=kt == KT - 1)
                    last.then_inc(k_made, 1)
                    pe.wait_ge(gate_ready, ff(b, w, c) + 1)
                    for i in range(BPC):
                        for kt in range(KT):
                            last = mm(pc[:, i // 2, (i % 2) * C:(i % 2 + 1) * C], x_r[c % 2][:, kt, i * P:(i + 1) * P],
                                      w_r[:, kt, :], start=kt == 0, stop=kt == KT - 1)
                    last.then_inc(gate_made, 1)
                    if c + 2 < NCH:
                        transposes(b, 2 * w, c + 2)
                    elif w == 0:
                        transposes(b, 1, c + 2 - NCH)
                    elif c == NCH - 1:
                        with pe.If(b < BATCH - 1):
                            transposes(b + 1, 0, 1)
                    pe.wait_ge(kact_ready, ff(b, w, c) + 1)
                    pe.wait_ge(ffn_read, ff(b, w, c) + 1)
                    for i in range(BPC):
                        for kt in range(KT):
                            last = mm(pd[:, i // 2, (i % 2) * C:(i % 2 + 1) * C], kact[c % 2][:, kt, i * P:(i + 1) * P],
                                      w_v[:, kt, :], start=kt == 0, stop=kt == KT - 1)
                    last.then_inc(ffn_made, 1)

            def value_tile(b, half, c, i):
                tile = half * NBLK + c * BPC + i
                if tile >= 2:
                    pe.wait_ge(v_stored, b * V_TILES + (tile - 1))
                for kt in range(KT):
                    last = mm(pd[:, tile % 2, :], xt[c][:, kt, i * P:(i + 1) * P],
                              w_val[:, kt, half * CH:(half + 1) * CH], start=kt == 0, stop=kt == KT - 1)
                last.then_inc(v_made, 1)

            def projections(b):
                for c in range(NCH):
                    turn = b * NCH + c
                    pe.wait_ge(xnt_copied, ln(b, 1, c) + 1 + 1)
                    if c == 0:
                        pe.wait_ge(k_relu, ff(b, 0, NCH - 1) + 1 + 1)
                        pe.wait_ge(gate_ready, ff(b, 0, NCH - 1) + 1 + 1)
                    else:
                        pe.wait_ge(norms_read, turn)
                    for what, (dst, wt, made) in enumerate(((pb, w_q, q_made), (pc, w_kc, kp_made))):
                        if dst is pc and c > 0:
                            pe.wait_ge(kp_copied, turn)
                        for mt in range(KT):
                            for kt in range(KT):
                                last = mm(dst[:, mt, :], wt[:, kt, mt * P:(mt + 1) * P], xt[c][:, kt, :],
                                          start=kt == 0, stop=kt == KT - 1)
                        last.then_inc(made, 1)
                        if c == 0 and what == 0:
                            pe.wait_ge(ffn_read, ff(b, 0, NCH - 1) + 1 + 1)
                        for i in range(2):
                            value_tile(b, 0, c, 2 * what + i)
                    pe.wait_ge(squares, turn * 2 + 2)
                    for what in range(2):
                        for ft in range(KT):
                            last = mm(pb[0:HEADS, what, :], head_rows[:, ft, :], sq[what][:, ft, :],
                                      start=ft == 0, stop=ft == KT - 1)
                    last.then_inc(norms_made, 1)
                    if c + 2 < NCH:
                        transposes(b, 1, c + 2)
                for c in range(NCH):
                    for i in range(BPC):
                        value_tile(b, 1, c, i)
                    if c == 0:
                        pe.wait_ge(over_ready, b + 1)
                        wait_alone(pe, norms_read, (b + 1) * NCH)
                        mm(pb[0:1, 0, 0:1], over[:], ones[0:HEADS, 0:1], start=True, stop=True)\
                            .then_inc(over_counted, 1)

            def score(n, par, u):
                c, j, off, _ = UNITS[u]
                pe.wait_ge(exped, n * NU + (u + 1))
                for h in range(2):
                    last = mm(scores[u % 2][:, h, off:], ks[par][0:QROWS, h, j * P:(j + 1) * P],
                              qs[par][0:QROWS, h, c * CH + off:(c + 1) * CH], start=True, stop=True)
                last.then_inc(scored, 1)

            def value(n, par, u):
                c, j, off, diag = UNITS[u]
                if u in FIRST:
                    pe.wait_ge(y_copied, n * NCH + (c + 1))
                if diag:
                    pe.wait_ge(masked, n * NDIAG + (DIAG[u] + 1))
                else:
                    pe.wait_ge(exped, n * NU + (u + 2 + 1))
                for h in range(2):
                    last = mm(pc[h * LAT:(h + 1) * LAT, c % 2, off:], vb[par][:, j, h * LAT:(h + 1) * LAT],
                              probs[u % NP_BUF][:, h, off:], start=u in FIRST, stop=u in LAST)
                last.then_inc(valued, 1)

            def denominators(n, g):
                last_unit = LAST[2 * g + 1]
                pe.wait_ge(summed, n * NU + (last_unit + NP_BUF + 1))
                pe.wait_ge(den_copied, n * GROUPS + (g + 1))
                for r in range(4):
                    last = mm(pd[32 * r:32 * (r + 1), g, :], ones[:], acc[2 * g + r // 2][:, r % 2, :],
                              start=True, stop=True)
                last.then_inc(den_made, 1)

            pe.wait_ge(ident_set, 1)
            pe.sem_inc(valued, NP_BUF)
            pe.sem_inc(den_made, GROUPS)
            pe.wait_ge(wk_loaded, 32)
            pe.wait_ge(wc_loaded, 32)
            for p in range(PAIRS):
                if p == PAIRS // 2:
                    transposes(0, 0, 0)
                for ct in range(KT):
                    mm(pc[:, ct, p * 2 * HD:(p + 1) * 2 * HD], wk_raw[:, p, ct * P:(ct + 1) * P], wc_pair[:],
                       start=True, stop=True)
            per = P // (2 * HD)
            for p in range(PAIRS):
                r = p % per
                last = mm(pb[32 * r:32 * (r + 1), 0, p // per:p // per + 1], wc_pair[:], b_k_raw[:, p:p + 1],
                          start=True, stop=True)
            last.then_inc(kc_done, 1)
            pe.wait_ge(w_loaded, 16 * 5)
            pe.wait_ge(consts_set, 3)
            transposes(0, 0, 1)
            pe.wait_ge(kc_copied, 2)

            with pe.Fori(0, BATCH) as b:
                ffn(b, 0)
                pe.wait_ge(attn_w_loaded, 16 * 6)
                projections(b)
                wait_alone(pe, flag_ready, b + 1)
                general = pe.value_load(flag[0:1, 0:1], min_val=0, max_val=HEADS)
                with pe.If(general > 0):
                    with pe.Fori(0, PAIRS) as p:
                        loads = len(PRODUCTS) * 32
                        wait_alone(pe, g_loaded, (b * PAIRS + p) * loads + loads)
                        for i in range(G_TURNS):
                            h, blk = divmod(i, NBLK)
                            pe.wait_ge(g_read, g_turn(b, p, i) + 1)
                            for k in range(blk // BPC + 1):
                                width = min(CH, (blk + 1) * P - k * CH)
                                last = mm(banks[k][:, 0:width], qs[0][0:QROWS - 1, h, blk * P:(blk + 1) * P],
                                          ks[0][0:QROWS - 1, h, k * CH:k * CH + width], start=True, stop=True)
                            last.then_inc(g_scored, 1)
                        wait_alone(pe, g_read, g_turn(b, p, G_TURNS) + 1)
                with pe.Else():
                    pe.sem_inc(g_scored, PAIRS * G_TURNS)
                wait_alone(pe, ones_rows, b * 2 + 2)
                def arrived(n_half, par):
                    pe.wait_ge(pair_loaded[par], n_half * LOADS + LOADS)

                arrived(b * (PAIRS // 2), 0)
                for u in range(PV_LAG):
                    score(b * PAIRS, 0, u)
                with pe.Fori(0, PAIRS // 2) as pp:
                    n0 = b * PAIRS + pp * 2
                    for v in range(2 * NU - PV_LAG):
                        value(n0 + v // NU, v // NU, v % NU)
                        s = v + PV_LAG
                        if s == NU:
                            arrived(b * (PAIRS // 2) + pp, 1)
                        score(n0 + s // NU, s // NU, s % NU)
                        if v == 5:
                            with pe.If(pp > 0):
                                denominators(n0 - 1, GROUPS - 1)
                        if v % NU == LAST[1] + 2:
                            denominators(n0 + v // NU, 0)
                        if v == NU + 5:
                            denominators(n0, GROUPS - 1)
                    with pe.If(pp < PAIRS // 2 - 1):
                        arrived(b * (PAIRS // 2) + pp + 1, 0)
                        for k in range(PV_LAG):
                            value(n0 + 1, 1, NU - PV_LAG + k)
                            score(n0 + 2, 0, k)
                    with pe.Else():
                        for k in range(PV_LAG):
                            value(n0 + 1, 1, NU - PV_LAG + k)
                denominators(b * PAIRS + (PAIRS - 1), GROUPS - 1)
                wait_alone(pe, exped, (b + 1) * (PAIRS * NU) + 2)
                wait_alone(pe, y_copied, (b + 1) * (PAIRS * NCH) + 2)
                wait_alone(pe, den_copied, (b + 1) * (PAIRS * GROUPS) + 2)
                for first in range(0, NBLK, O_BANKS):
                    blks = range(first, min(first + O_BANKS, NBLK))
                    for p in range(PAIRS):
                        if first == 0:
                            pe.wait_ge(y_scaled, b * PAIRS + (p + 1) + 1)
                        for blk in blks:
                            if p == 0 and first > 0:
                                pe.wait_ge(o_added, b * NBLK + (blk - O_BANKS + 1))
                            last = mm(banks[2 + blk % O_BANKS][:, 0:C], slots[:, p, blk * P:(blk + 1) * P],
                                      w_o[:, p, :], start=p == 0, stop=p == PAIRS - 1)
                            if p == PAIRS - 1:
                                last.then_inc(o_made, 1)
                        if first > 0 and p == PAIRS - 2:
                            transposes(b, 2, first // O_BANKS - 1)
                ffn(b, 1)

        @block.scalar
        def _(act):
            A = nc.scalar.activation

            def copy_xnt(b, st, c):
                act.wait_ge(xnt_made, ln(b, st, c) + 1)
                act.wait_ge(mixed, ff(b, st // 2, c) + 1 if st != 1 else ff(b, 1, 0) + 1)
                dst = xt[c] if st == 1 else xnt[c % 2][:, :, 1:CH + 1]
                A(dst, pa[:], ACT.Copy).then_inc(xnt_copied, 1)

            def ffn(b, w):
                for c in range(NCH):
                    if w == 1 and c == NCH - 1:
                        with act.If(b < BATCH - 1):
                            copy_xnt(b + 1, 0, 0)
                    act.wait_ge(k_made, ff(b, w, c) + 1)
                    if c >= 2:
                        act.wait_ge(ffn_made, ff(b, w, c - 1))
                    A(kact[c % 2][:], pb[:], ACT.Relu).then_inc(k_relu, 1)
                    act.wait_ge(k_relu, ff(b, w, c) + 1 + 1)
                    A(kact[c % 2][:], kact[c % 2][:], ACT.Square).then_inc(kact_ready, 1)
                    act.wait_ge(gate_made, ff(b, w, c) + 1)
                    if c >= 2:
                        act.wait_ge(ffn_read, ff(b, w, c - 1) + 1)
                    A(gate[c % 2].rearrange("p (a b) c -> p a (b c)", a=2), pc[:], ACT.Sigmoid).then_inc(gate_ready, 1)
                    if c + 2 < NCH:
                        copy_xnt(b, 2 * w, c + 2)
                    elif w == 0:
                        copy_xnt(b, 1, c + 2 - NCH)
                    elif c == NCH - 1:
                        with act.If(b < BATCH - 1):
                            copy_xnt(b + 1, 0, 1)

            def y_copy(n, p, c):
                act.wait_ge(valued, n * NU + (LAST[c] + NP_BUF + 1))
                dst = slots[:, bass.ds(p, 1), c * CH:(c + 1) * CH].rearrange("p o n -> p (o n)")
                A(dst, pc[:, c % 2, :], ACT.Copy).then_inc(y_copied, 1)

            def den_copy(n, g):
                act.wait_ge(den_made, n * GROUPS + (g + GROUPS + 1))
                act.wait_ge(den_sent, n * (16 * GROUPS) + 48)
                A(den[:, g, :], pd[:, g, :], ACT.Copy).then_inc(den_copied, 1)

            for s in (xnt_copied, gate_ready, k_relu):
                act.sem_inc(s, 1)
            act.sem_inc(exped, 2)
            act.sem_inc(y_copied, 2)
            act.sem_inc(den_copied, 2)
            copy_xnt(0, 0, 0)
            act.wait_ge(kc_done, 1)
            A(w_kc[:], pc[:, :, 0:C], ACT.Copy).then_inc(kc_copied, 1)
            A(b_kc[:], pb[:, 0, 0:KT], ACT.Copy).then_inc(kc_copied, 1)
            act.wait_ge(kc_copied, 2)
            copy_xnt(0, 0, 1)

            with act.Fori(0, BATCH) as b:
                ffn(b, 0)
                act.wait_ge(attn_w_loaded, 16 * 6)
                for c in range(NCH):
                    turn = b * NCH + c
                    for what, (src, dst, bias, made, copied, high, saved) in enumerate((
                            (pb, qf, b_q, q_made, q_copied, q_parts, q_saved),
                            (pc, kf, b_kc, kp_made, kp_copied, k_parts, k_saved))):
                        act.wait_ge(made, turn + 1)
                        if c > 0:
                            act.wait_ge((q_split, k_split)[what], turn)
                        for mt in range(KT):
                            last = A(dst[:, mt, :], src[:, mt, :], ACT.Identity, bias=bias[:, mt:mt + 1])
                        last.then_inc(copied, 1)
                        act.wait_ge(copied, turn + 1)
                        if c == 0:
                            act.wait_ge(ffn_added, ff(b, 1, 0))
                        act.wait_ge(saved, turn * 16 + 16)
                        A(high[:, 0], dst, ACT.Copy).then_inc(rounded, 1)
                    if c > 0:
                        act.wait_ge(norms_made, turn)
                    else:
                        act.wait_ge(ffn_read, ff(b, 1, 0) + 1)
                    for what, (src, copied) in enumerate(((qf, q_copied), (kf, kp_copied))):
                        act.wait_ge(copied, turn + 1)
                        A(sq[what], src, ACT.Square).then_inc(squares, 1)
                    if c + 2 < NCH:
                        copy_xnt(b, 1, c + 2)
                act.wait_ge(bound_inputs, b + 1)
                A(qnorm, qnorm, ACT.Sqrt, scale=kmax[:, 0:1]).then_inc(bound_ready, 1)

                with act.Fori(0, PAIRS // 2) as pp:
                    n0 = b * PAIRS + pp * 2

                    for s in range(2 * NU):
                        par, u = divmod(s, NU)
                        n, off = n0 + par, UNITS[u][2]
                        act.wait_ge(scored, n * NU + (u + 1))
                        act.wait_ge(valued, n * NU + (u + 1))
                        act.wait_ge(summed, n * NU + (u + 1))
                        A(probs[u % NP_BUF][:, :, off:], scores[u % 2][:, :, off:], ACT.Exp,
                          scale=SCALE).then_inc(exped, 1)
                        for c in range(NCH - 1):
                            if u == LAST[c] + 4:
                                y_copy(n, pp * 2 + par, c)
                        if u == LAST[1] + 8:
                            den_copy(n, 0)
                        if s == 4:
                            with act.If(pp > 0):
                                y_copy(n0 - 1, the_pair_before(pp), NCH - 1)
                        if s == 9:
                            with act.If(pp > 0):
                                den_copy(n0 - 1, GROUPS - 1)
                        if s == NU + 4:
                            y_copy(n0, pp * 2, NCH - 1)
                        if s == NU + 9:
                            den_copy(n0, GROUPS - 1)
                y_copy(b * PAIRS + (PAIRS - 1), PAIRS - 1, NCH - 1)
                den_copy(b * PAIRS + (PAIRS - 1), GROUPS - 1)
                for c in range(2):
                    copy_xnt(b, 2, c)
                ffn(b, 1)

        @block.gpsimd
        def _(pool):
            g = nc.gpsimd
            g.memset(wc_pair[:], 0.0).then_inc(wc_zeroed, 1)
            pool.sem_inc(y_scaled, 1)
            g.memset(ident[:], 0.0).then_inc(pool_step, 1)
            g.memset(ones[:], 1.0).then_inc(consts_set, 1)
            g.memset(eps_half[:], -0.5).then_inc(pool_step, 1)
            g.memset(head_rows[:], 1.0).then_inc(pool_step, 1)
            g.memset(tri[:], 0.0).then_inc(pool_step, 1)
            pool.wait_ge(pool_step, 4)
            g.affine_select(out=ident[:], in_=ident[:], compare_op=ALU.not_equal, fill=1.0, base=0,
                            pattern=[[-1, P]], channel_multiplier=1).then_inc(ident_set, 1)
            g.affine_select(out=tri[:], in_=tri[:], compare_op=ALU.is_ge, fill=MASKED, base=0,
                            pattern=[[-1, P]], channel_multiplier=1).then_inc(consts_set, 1)
            hr = head_rows[:]
            g.affine_select(out=hr, in_=hr, compare_op=ALU.is_ge, fill=0.0, base=0,
                            pattern=[[P, KT], [-HD, HEADS]], channel_multiplier=1).then_inc(pool_step, 1)
            pool.wait_ge(pool_step, 5)
            g.affine_select(out=hr, in_=hr, compare_op=ALU.is_ge, fill=0.0, base=HD - 1,
                            pattern=[[-P, KT], [HD, HEADS]], channel_multiplier=-1).then_inc(consts_set, 1)

            def ln_power(b, st, c):
                turn = ln(b, st, c)
                wait_alone(pool, stats_ready, turn + 1)
                g.tensor_scalar(rstd[:, c % 2, :], mv[:, c % 2, :, 1], EPS, None, ALU.add).then_inc(pool_step, 1)
                pool.wait_ge(pool_step, turn + 6)
                g.tensor_tensor(rstd[:, c % 2, :], rstd[:, c % 2, :], eps_half[:], ALU.pow).then_inc(rstd_ready, 1)

            for c in range(2):
                ln_power(0, 0, c)
            with pool.Fori(0, BATCH) as b:
                for st in range(2):
                    for c in range(2 if st == 0 else 0, NCH):
                        ln_power(b, st, c)
                pool.wait_ge(xn_ready, ln(b, 1, NCH - 1) + 1)
                pool.wait_ge(attn_w_loaded, 16 * 6)
                for i in range(NBLK):
                    g.tensor_tensor(x_sb[:, i, :], x_sb[:, i, :], b_o[:], ALU.add).then_inc(bo_added, 1)

                wait_alone(pool, k_saved, b * (16 * NCH) + 16 * NCH + 16)
                wait_alone(pool, q_saved, b * (16 * NCH) + 16 * NCH + 16)
                wait_alone(pool, bo_added, (b + 1) * NBLK)
                for i in range(2):
                    g.memset(ks[i][QROWS - 1:QROWS, :, :], 1.0).then_inc(ones_rows, 1)
                    wait_alone(pool, ones_rows, b * 2 + (i + 1))

                def scale_y(n, p):
                    pool.wait_ge(rden_back, n * 32 + 32)
                    pool.wait_ge(y_copied, n * NCH + (NCH + 2))
                    y = slots[:, bass.ds(p, 1), :].rearrange("p o n -> p (o n)")
                    g.tensor_tensor(y, y, rden[:].rearrange("p a b -> p (a b)"), ALU.mult).then_inc(y_scaled, 1)

                with pool.Fori(0, PAIRS // 2) as pp:
                    n0 = b * PAIRS + pp * 2
                    for par in range(2):
                        for u, (c, j, off, diag) in enumerate(UNITS):
                            if diag:
                                wait_alone(pool, exped, (n0 + par) * NU + (u + 3))
                                tile = probs[u % NP_BUF][:, :, off:off + P]
                                g.affine_select(out=tile, in_=tile, compare_op=ALU.is_ge, fill=0.0, base=0,
                                                pattern=[[0, 2], [1, P]], channel_multiplier=-1).then_inc(masked, 1)
                            if u == LAST[2]:
                                if par == 0:
                                    with pool.If(pp > 0):
                                        scale_y(n0 - 1, the_pair_before(pp))
                                else:
                                    scale_y(n0, pp * 2)
                scale_y(b * PAIRS + (PAIRS - 1), PAIRS - 1)
                for c in range(NCH):
                    ln_power(b, 2, c)
                with pool.If(b < BATCH - 1):
                    for c in range(2):
                        ln_power(b + 1, 0, c)

        @block.vector
        def _(dve):
            v = nc.vector
            count = [0]

            def link(b, ins, alone=False):
                count[0] += 1
                ins.then_inc(dve_step, 1)
                (wait_alone if alone else type(dve).wait_ge)(dve, dve_step, b * STEPS + count[0])

            def ln_stats(b, st, c, ahead=False):
                if st == 0:
                    dve.wait_ge(x_loaded[c], b * 16 + 16)
                elif st == 1:
                    dve.wait_ge(ffn_added, ff(b, 0, c) + 1)
                else:
                    dve.wait_ge(o_added, b * NBLK + (c + 1) * BPC)
                for i in range(BPC):
                    last = v.bn_stats(stats[:, c % 2, i, :], x_sb[:, c * BPC + i, :])
                link(b - 1 if ahead else b, last, alone=True)
                for i in range(BPC):
                    last = v.bn_aggr(mv[:, c % 2, i, :], stats[:, c % 2, i, :])
                last.then_inc(stats_ready, 1)

            def ln_apply(b, st, c):
                turn = ln(b, st, c)
                dve.wait_ge(rstd_ready, turn + 1)
                if c >= 2 or st > 0:
                    dve.wait_ge(xnt_made, turn - 1)
                for i in range(BPC):
                    last = v.tensor_scalar(xn[c % 2][:, i, :], x_sb[:, c * BPC + i, :], mv[:, c % 2, i, 0:1],
                                           rstd[:, c % 2, i:i + 1], ALU.subtract, ALU.mult)
                last.then_inc(xn_ready, 1)

            def mix(b, w, c, ahead=False):
                cur, old = xnt[c % 2], xnt[(c + 1) % 2]
                now = b - 1 if ahead else b
                dve.wait_ge(xnt_copied, ln(b, 2 * w, c) + 1 + 1)
                if c == 0:
                    link(now, v.memset(cur[:, :, 0:1], 0.0))
                else:
                    link(now, v.tensor_copy(cur[:, :, 0:1], old[:, :, CH:CH + 1]))
                if c >= 2 or ahead:
                    dve.wait_ge(gate_made, ff(b, w, c - 1))
                link(now, v.tensor_tensor(diff, cur[:, :, 1:CH + 1], cur[:, :, 0:CH], ALU.subtract))
                for dst, mu in ((x_r, mur), (x_k, muk)):
                    for kt in range(KT):
                        last = v.scalar_tensor_tensor(dst[c % 2][:, kt, :], diff[:, kt, :], mu[:, kt:kt + 1],
                                                      cur[:, kt, 0:CH], ALU.mult, ALU.add)
                last.then_inc(mixed, 1)

            def add_ffn(b, w, c):
                dve.wait_ge(ffn_made, ff(b, w, c) + 1)
                dve.wait_ge(gate_ready, ff(b, w, c) + 1 + 1)
                if c > 0:
                    dve.wait_ge(ffn_added, ff(b, w, c))
                v.scalar_tensor_tensor(prod, pd[:].rearrange("p a (b c) -> p (a b) c", c=C), 0.5,
                                       gate[c % 2], ALU.mult, ALU.mult).then_inc(ffn_read, 1)
                dve.wait_ge(ffn_read, ff(b, w, c) + 1 + 1)
                xc = x_sb[:, c * BPC:(c + 1) * BPC, :]
                ins = v.tensor_tensor(xc, xc, prod, ALU.add)
                ins.then_inc(ffn_added, 1)

            def normalise(b, st, c, ahead=False):
                ln_stats(b, st, c, ahead)
                ln_apply(b, st, c)

            def ffn(b, w):
                normalise(b, 2 * w, 2)
                for c in range(NCH):
                    if c + 1 < NCH:
                        mix(b, w, c + 1)
                    if c + 3 < NCH:
                        normalise(b, 2 * w, c + 3)
                    elif w == 0:
                        normalise(b, 1, c + 3 - NCH)
                    elif c >= 2:
                        with dve.If(b < BATCH - 1):
                            normalise(b + 1, 0, c - 2, ahead=True)
                            if c == NCH - 1:
                                mix(b + 1, 0, 0, ahead=True)
                    add_ffn(b, w, c)

            def store_v(b, half, c, i):
                tile, blk, per = half * NBLK + c * BPC + i, c * BPC + i, PAIRS // 2
                dve.wait_ge(v_made, b * V_TILES + (tile + 1))
                dst = slots[:, half * per:(half + 1) * per, blk * P:(blk + 1) * P]
                v.tensor_tensor(dst, pd[:, tile % 2, :].rearrange("p (a b) -> p a b", a=per),
                                b_val[:, half * CH:(half + 1) * CH].rearrange("p (a b) -> p a b", a=per),
                                ALU.add).then_inc(v_stored, 1)

            dve.sem_inc(summed, NP_BUF)
            for s in (ffn_read, mixed, g_read):
                dve.sem_inc(s, 1)
            normalise(0, 0, 0)
            normalise(0, 0, 1)
            dve.wait_ge(w_loaded, 16 * 5)
            dve.wait_ge(consts_set, 3)
            mix(0, 0, 0)
            lead = count[0]
            with dve.Fori(0, BATCH) as b:
                ffn(b, 0)
                dve.wait_ge(attn_w_loaded, 16 * 6)
                for c in range(NCH):
                    turn = b * NCH + c
                    if c == 0:
                        normalise(b, 1, NCH - 1)

                    for what, (src, parts, split) in enumerate(((qf, q_parts, q_split), (kf, k_parts, k_split))):
                        dve.wait_ge(rounded, turn * 2 + (what + 1))
                        link(b, v.tensor_tensor(rest[what][:], src, parts[:, 0], ALU.subtract))
                        link(b, v.tensor_copy(parts[:, 1], rest[what][:]))
                        v.tensor_tensor(parts[:, 2], rest[what][:], parts[:, 1], ALU.subtract).then_inc(split, 1)
                        if what == 1:
                            dve.wait_ge(norms_made, turn + 1)
                            v.tensor_copy(qnorm[:, c * CH:(c + 1) * CH], pb[0:HEADS, 0, :])
                            v.tensor_reduce(kmax4[:, c:c + 1], pb[0:HEADS, 1, :], AX.X, ALU.max).then_inc(norms_read, 1)
                        for i in range(2):
                            store_v(b, 0, c, 2 * what + i)
                dve.wait_ge(norms_read, (b + 1) * NCH)
                v.tensor_reduce(kmax[:], kmax4[:], AX.X, ALU.max).then_inc(bound_inputs, 1)
                for i in range(2):
                    store_v(b, 1, 0, i)
                dve.wait_ge(bound_ready, b + 1)
                v.tensor_scalar(shift, qnorm, -MARGIN, None, ALU.mult).then_inc(shift_ready, 1)
                link(b, v.tensor_reduce(kmax4[:, 0:1], qnorm, AX.X, ALU.max))
                v.tensor_scalar(over[:], kmax4[:, 0:1], SAFE, None, ALU.is_gt).then_inc(over_ready, 1)
                for i in range(2, BPC):
                    store_v(b, 1, 0, i)
                dve.wait_ge(over_counted, b + 1)
                v.tensor_copy(flag[:], pb[0:1, 0, 0:1]).then_inc(flag_ready, 1)

                wait_alone(dve, flag_ready, b + 1)
                for c in range(1, NCH):
                    for i in range(BPC):
                        store_v(b, 1, c, i)
                general = dve.value_load(flag[0:1, 0:1], min_val=0, max_val=HEADS)
                with dve.If(general > 0):
                    with dve.Fori(0, PAIRS) as p:
                        wait_alone(dve, g_sent, (b * PAIRS + p) * 16 + 16)
                        for i in range(G_TURNS):
                            h, blk = divmod(i, NBLK)
                            k, low = blk // BPC, blk % BPC * P
                            turn = g_turn(b, p, i)

                            def g_link(ins, step):
                                ins.then_inc(g_step, 1)
                                dve.wait_ge(g_step, turn * G_STEPS + step)

                            g_link(v.memset(g_part[:], MASKED), 1)
                            dve.wait_ge(g_scored, turn + 1)
                            for full in range(k):
                                v.tensor_reduce(g_part[:, full:full + 1], banks[full][:], AX.X, ALU.max)
                            if low:
                                v.tensor_reduce(g_part[:, k:k + 1], banks[k][:, 0:low], AX.X, ALU.max)
                            g_link(v.tensor_tensor(g_diag, banks[k][:, low:low + P], tri[:], ALU.add), 2)
                            g_link(v.tensor_reduce(g_part[:, NCH:NCH + 1], g_diag, AX.X, ALU.max), 3)
                            g_link(v.tensor_reduce(g_top[:], g_part[:], AX.X, ALU.max), 4)
                            last = v.tensor_scalar(g_shift[:, h, blk:blk + 1], g_top[:], -1.0, None, ALU.mult)
                            last.then_inc(g_read, 1)
                        dve.wait_ge(g_read, g_turn(b, p, G_TURNS) + 1)
                        dve.sem_inc(g_max, 1)
                with dve.Else():
                    dve.sem_inc(g_step, PAIRS * G_TURNS * G_STEPS)
                    dve.sem_inc(g_read, PAIRS * G_TURNS)
                    dve.sem_inc(g_max, PAIRS)

                def invert(n):
                    dve.wait_ge(den_back, n * 16 + 16)
                    v.reciprocal(rden_c[:], den_c[:]).then_inc(rden_made, 1)

                with dve.Fori(0, PAIRS // 2) as pp:
                    n0 = b * PAIRS + pp * 2
                    for par in range(2):
                        n = n0 + par
                        for u, (c, j, off, diag) in enumerate(UNITS):
                            if diag:
                                dve.wait_ge(masked, n * NDIAG + (DIAG[u] + 1))
                            else:
                                dve.wait_ge(exped, n * NU + (u + 3))
                            if u in FIRST:
                                dve.wait_ge(den_made, n * GROUPS + (c // 2 + 1))
                                v.tensor_copy(acc[c][:], probs[u % NP_BUF][:]).then_inc(summed, 1)
                            else:
                                dve.wait_ge(summed, n * NU + (u + NP_BUF))
                                a = acc[c][:, :, off:]
                                v.tensor_tensor(a, a, probs[u % NP_BUF][:, :, off:], ALU.add).then_inc(summed, 1)
                            if u == 16:
                                if par == 0:
                                    with dve.If(pp > 0):
                                        invert(n0 - 1)
                                else:
                                    invert(n0)
                invert(b * PAIRS + (PAIRS - 1))
                dve.wait_ge(bo_added, (b + 1) * NBLK)
                for blk in range(NBLK):
                    dve.wait_ge(o_made, b * NBLK + (blk + 1))
                    v.tensor_tensor(x_sb[:, blk, :], x_sb[:, blk, :], banks[2 + blk % O_BANKS][:, 0:C],
                                    ALU.add).then_inc(o_added, 1)
                    if blk in (O_BANKS - 1, 2 * O_BANKS - 1):
                        normalise(b, 2, blk // O_BANKS)
                    if blk == 2 * O_BANKS - 1:
                        mix(b, 1, 0)
                ffn(b, 1)
            assert count[0] == STEPS + lead, count[0] - lead


STEPS = 45
_IN = ["x", "ffn_wr", "ffn_wk", "ffn_wv", "mu_r", "mu_k", "wq", "bq", "wk_t", "bk", "wc_t", "wv", "bv", "wo", "bo"]


def _layout(inputs):
    import numpy as np
    a = {k.removeprefix("L0_"): np.asarray(v) for k, v in inputs.items()}

    def rows(w, n=128):
        return np.ascontiguousarray(w.reshape(-1, n, w.shape[-1]).transpose(1, 0, 2))

    def cols(v, n=128):
        return np.ascontiguousarray(v.reshape(-1, n).T)

    return {
        "x": a["attn_x"].reshape(-1, a["attn_x"].shape[-1]),
        "ffn_wr": rows(a["ffn_W_r"].T), "ffn_wk": rows(a["ffn_W_k"].T), "ffn_wv": rows(a["ffn_W_v"].T),
        "mu_r": cols(a["ffn_mu_r"]), "mu_k": cols(a["ffn_mu_k"]),
        "wq": rows(a["attn_Wq"]), "bq": cols(a["attn_bq"]),
        "wk_t": rows(a["attn_Wk"].T), "bk": cols(a["attn_bk"]), "wc_t": np.ascontiguousarray(a["attn_Wc"].T),
        "wv": rows(a["attn_Wv"]), "bv": a["attn_bv"].reshape(1, -1), "wo": rows(a["attn_Wo"]),
        "bo": a["attn_bo"].reshape(1, -1),
    }


def kernel(**inputs):
    import numpy as np
    import concourse.bacc as bacc
    from concourse.bass_utils import run_bass_kernel_spmd

    batch, t, c = inputs["L0_attn_x"].shape
    heads = 16
    arrays = {f"in_{k}": v for k, v in _layout(inputs).items()}
    nc = bacc.Bacc("TRN2", target_bir_lowering=False, num_devices=1)
    ins = [nc.dram_tensor(f"in_{k}", arrays[f"in_{k}"].shape, mybir.dt.from_np(arrays[f"in_{k}"].dtype),
                          kind="ExternalInput").ap() for k in _IN]
    out = nc.dram_tensor("out", (batch * t, c), mybir.dt.float32, kind="ExternalOutput").ap()
    qk = nc.dram_tensor("qk_scratch", (batch, 2, 3, c, t), mybir.dt.bfloat16, kind="Internal").ap()
    shift = nc.dram_tensor("shift_scratch", (batch, heads, t), mybir.dt.bfloat16, kind="Internal").ap()
    den = nc.dram_tensor("den_scratch", (2, 4, 512), mybir.dt.float32, kind="Internal").ap()
    rden = nc.dram_tensor("rden_scratch", (2, 4, 512), mybir.dt.float32, kind="Internal").ap()
    macaron_block(nc, ins[0], out, *ins[1:], qk, shift, den, rden)
    r = run_bass_kernel_spmd(nc, [arrays], core_ids=[0])
    return np.asarray(r.results[0]["out"]).reshape(batch, t, c)
```

```python
import concourse.bass as bass
from concourse import mybir
from contextlib import ExitStack


def macaron_block(nc, x, out, ffn_wr, ffn_wk, ffn_wv, mu_r, mu_k, wq, bq, wk_t, bk, wc_t, wv, bv, wo, bo,
                  qk_scratch, wqk_low_scratch, wval_low_scratch, wo_scratch, shift_scratch, den_scratch, rden_scratch):
    fp32, f32r, bf16, i32 = mybir.dt.float32, mybir.dt.float32r, mybir.dt.bfloat16, mybir.dt.int32
    ALU, ACT, AX = mybir.AluOpType, mybir.ActivationFunctionType, mybir.AxisListType

    P = 128
    C = wq.shape[2]
    BATCH = qk_scratch.shape[0]
    T = x.shape[0] // BATCH
    KT = C // P
    CH = 512
    NCH = T // CH
    BPC = CH // P
    NBLK = T // P
    HEADS, LAT = 16, 64
    HD = C // HEADS
    PAIRS = HEADS // 2
    PRODUCTS = ((0, 0), (0, 1), (0, 2), (1, 0), (1, 1), (2, 0))
    QROWS = len(PRODUCTS) * HD + 1
    SCALE = LAT ** -0.5
    EPS = 1e-5
    SAFE = 35.0 / SCALE
    MARGIN = 1.01
    MASKED = -3.0e38

    UNITS = []
    for c in range(NCH):
        UNITS += [(c, j, 0, False) for j in range(BPC * c)]
        UNITS += [(c, BPC * c + i, P * i, True) for i in range(BPC)]
    NU = len(UNITS)
    FIRST = [u for u in range(NU) if u == 0 or UNITS[u - 1][0] != UNITS[u][0]]
    LAST = [u for u in range(NU) if u == NU - 1 or UNITS[u + 1][0] != UNITS[u][0]]
    DIAG = [sum(UNITS[v][3] for v in range(u)) for u in range(NU)]
    NDIAG = NCH * BPC
    NP_BUF = 4
    PV_LAG = 3
    GROUPS = NCH // 2
    assert NU % NP_BUF == 0 and NU % 2 == 0

    ctx = ExitStack()
    with ctx:
        def sb(name, shape, dt=fp32):
            return ctx.enter_context(nc.sbuf_tensor(name, shape, dt))

        def region(name, size):
            sb(name, [P, size // 4])
            return nc.sbuf_base - size

        def place(name, shape, dt, at):
            return nc.alloc_sbuf_tensor_at(name, shape, dt, offset=at)

        def sem(name):
            return ctx.enter_context(nc.semaphore(name))

        w_r, w_k, w_v = sb("w_r", [P, KT, C]), sb("w_k", [P, KT, C]), sb("w_v", [P, KT, C])
        mur, muk = sb("mur", [P, KT]), sb("muk", [P, KT])
        w_q, b_q = sb("w_q", [P, KT, C], f32r), sb("b_q", [P, KT])
        w_kc, b_kc = sb("w_kc", [P, KT, C], f32r), sb("b_kc", [P, KT])
        w_val, b_val = sb("w_val", [P, KT, HEADS * LAT], f32r), sb("b_val", [P, HEADS * LAT])
        wo_bytes = region("wo_bytes", 4 * PAIRS * C)
        w_o, b_o = place("w_o", [P, PAIRS, C], f32r, wo_bytes), sb("b_o", [P, C])
        w_val_low = place("w_val_low", [P, KT, HEADS * LAT], f32r, wo_bytes)
        b_k_raw = sb("b_k_raw", [P, PAIRS])
        wc_pair = sb("wc_pair", [P, 2 * HD])
        ident = sb("ident", [P, P])
        ones = sb("ones", [P, 32])
        head_rows = sb("head_rows", [P, KT, HEADS], bf16)
        eps_half = sb("eps_half", [P, BPC])
        tri = sb("tri", [P, P])

        x_sb = sb("x_sb", [P, NBLK, C])
        SLOT = 4 * NBLK * P
        slots_bytes = region("slots_bytes", PAIRS * SLOT)
        slots = place("slots", [P, PAIRS, NBLK * P], fp32, slots_bytes)
        y_low = place("y_low", [P, PAIRS, NBLK * P], f32r, slots_bytes)
        stats = sb("stats", [P, 2, BPC, 6])
        mv = sb("mv", [P, 2, BPC, 2])
        rstd = sb("rstd", [P, 2, BPC])
        norm_max = sb("norm_max", [HEADS, 2, NCH])
        row_max, over = sb("row_max", [HEADS, 2]), sb("over", [HEADS, 1])
        flag = sb("flag", [1, 1], i32)
        exp_table = sb("exp_table", [1, 1])

        QK = 2 * 2 * T
        qk_bytes = region("qk_bytes", 4 * QK)
        qs = [place(f"qs{i}", [P, 2, T], bf16, qk_bytes + i * QK) for i in range(2)]
        ks = [place(f"ks{i}", [P, 2, T], bf16, qk_bytes + (3 - i) * QK) for i in range(2)]
        w_o_low = place("w_o_low", [P, PAIRS, C], f32r, qk_bytes + 3 * QK)
        TILE = 4 * KT * CH
        XNT = -(-4 * KT * (CH + 2) // 32) * 32
        v_bytes = region("v_bytes", max(4 * 2 * NBLK * P, 2 * (XNT + TILE)))
        vb = [place(f"vb{i}", [P, NBLK, P], fp32, v_bytes + i * 4 * NBLK * P) for i in range(2)]
        probs_bytes = region("probs_bytes", NP_BUF * 4 * 2 * CH)
        probs = [place(f"probs{i}", [P, 2, CH], fp32, probs_bytes + i * 4 * 2 * CH) for i in range(NP_BUF)]
        acc_bytes = region("acc_bytes", NCH * 4 * 2 * CH)
        acc = [place(f"acc{i}", [P, 2, CH], fp32, acc_bytes + i * 4 * 2 * CH) for i in range(NCH)]
        den_bytes = region("den_bytes", 4 * GROUPS * CH)
        den = place("den", [P, GROUPS, CH], fp32, den_bytes)
        w_q_low = place("w_q_low", [P, KT, C], f32r, den_bytes)
        w_kc_low = place("w_kc_low", [P, KT, C], f32r, den_bytes + 4 * KT * C)
        den_c, rden_c = sb("den_c", [P, 2 * T // P]), sb("rden_c", [P, 2 * T // P])
        rden = sb("rden", [P, NCH, CH])

        O_PASSES = ((0, 2 * BPC), (2 * BPC, 3 * BPC), (3 * BPC, 4 * BPC))
        O_BANK = (2, 3, 4, 5, 6, 7, 0, 1) + (2, 3, 4, 5) + (6, 7, 4, 5)
        O_BEFORE = [max((v for v in range(u) if O_BANK[v] == O_BANK[u]), default=None) for u in range(NBLK)]
        over_qk = 3 * QK // (4 * P * 2 * BPC)
        PLACES = (((qk_bytes, over_qk), (v_bytes, PAIRS - over_qk)), ((probs_bytes, PAIRS),), ((acc_bytes, PAIRS),))
        y_high_tiles = [[place(f"y_high{k}_{at}_{i}", [P, (end - first) * P], f32r, at + i * 4 * P * (end - first))
                         for at, n in PLACES[k] for i in range(n)] for k, (first, end) in enumerate(O_PASSES)]

        def y_high(k, p):
            return y_high_tiles[k][p][:]

        Y_SPLITS = [(k, p) for k in range(2) for p in range(PAIRS - 1)] + [(0, PAIRS - 1)]
        Y_SPLITS += [(1, PAIRS - 1)] + [(2, p) for p in range(PAIRS)]
        EARLY = 2
        NYS = len(Y_SPLITS)

        def view(t, k, n, shape):
            flat = t[:].rearrange("p a b -> p (a b)")[:, 2 * k:2 * (k + n)].bitcast(fp32)
            return flat.rearrange("p (a b) -> p a b", a=shape[0])
        W = CH * KT
        xn = [view(qs[0], i * W, W, (BPC, C)) for i in range(2)]
        x_r = [view(qs[1], i * W, W, (KT, CH)) for i in range(2)]
        x_k = [rden[:, i * KT:(i + 1) * KT, :] for i in range(2)]
        diff = view(ks[1], 0, W, (KT, CH))
        prod = view(ks[1], W, W, (BPC, C))
        kact = [probs[i] for i in range(2)]
        gate = [probs[2 + i][:].rearrange("p a (b c) -> p (a b) c", b=BPC // KT) for i in range(2)]
        xnt_at = [v_bytes + i * (XNT + TILE) for i in range(2)]
        xnt = [place(f"xnt{i}", [P, KT, CH + 2], fp32, xnt_at[i])[:] for i in range(2)]
        x_high = [place(f"x_high{i}", [P, KT, CH], f32r, acc_bytes + i * TILE) for i in range(NCH)]
        x_low = [place(f"x_low{i}", [P, KT, CH], f32r, xnt_at[i % 2] + (XNT if i < 2 else 0)) for i in range(NCH)]
        qf, kf = view(qs[1], 0, W, (KT, CH)), view(qs[1], W, W, (KT, CH))
        q_parts = ks[0][:].rearrange("p a b -> p (a b)")[:, 0:3 * W].rearrange("p (s a b) -> p s a b", s=3, a=KT)
        k_parts = ks[1][:].rearrange("p a b -> p (a b)")[:, 0:3 * W].rearrange("p (s a b) -> p s a b", s=3, a=KT)
        rest = [probs[0], probs[1]]
        sq = [probs[2][:].rearrange("p a b -> p (a b)")[:, i * (W // 2):(i + 1) * (W // 2)].bitcast(bf16)
              .rearrange("p (a b) -> p a b", a=KT) for i in range(2)]
        qnorm = rden[0:HEADS].rearrange("p a b -> p (a b)")
        shift = probs[3][0:HEADS].rearrange("p a b -> p (a b)").bitcast(bf16)
        raw = slots[:].rearrange("p a b -> p (a b)")
        wk_raw = raw[:, 0:PAIRS * C].rearrange("p (a b) -> p a b", a=PAIRS)
        wv_raw = raw[:, NBLK * P:NBLK * P + KT * HEADS * LAT].rearrange("p (a b) -> p a b", a=KT)
        WO_AT = (PAIRS - 2) * NBLK * P
        wo_raw = raw[:, WO_AT:WO_AT + PAIRS * C].rearrange("p (a b) -> p a b", a=PAIRS)
        wo_parts = [place(f"wo_part{i}", [P, PAIRS, C], f32r, slots_bytes + (PAIRS - 3 + i) * SLOT) for i in range(2)]
        wq_raw = raw[:, 2 * NBLK * P:2 * NBLK * P + KT * C].rearrange("p (a b) -> p a b", a=KT)

        pa, pb, pc, pd = (ctx.enter_context(nc.psum_tensor(n, [P, 2, CH], fp32)) for n in ("pa", "pb", "pc", "pd"))
        scores = [pa, pb]
        banks = [t[:, i, :] for t in (pa, pb, pc, pd) for i in range(2)]

        w_loaded, wc_zeroed, wc_loaded, wk_loaded = sem("w_loaded"), sem("wc_zeroed"), sem("wc_loaded"), sem("wk_loaded")
        raw_w_loaded, bias_loaded, wo_loaded = sem("raw_w_loaded"), sem("bias_loaded"), sem("wo_loaded")
        w_high, w_low, low_there = sem("w_high"), sem("w_low"), sem("low_there")
        x_high_made = sem("x_high_made")
        wo_raw_loaded, wo_high_made, wo_low_made, wo_saved = (
            sem("wo_raw_loaded"), sem("wo_high_made"), sem("wo_low_made"), sem("wo_saved"))
        y_high_made, y_low_made, y_tail_scaled = sem("y_high_made"), sem("y_low_made"), sem("y_tail_scaled")
        consts_set, ident_set, kc_done, kc_copied = sem("consts_set"), sem("ident_set"), sem("kc_done"), sem("kc_copied")
        x_loaded = [sem(f"x_loaded{c}") for c in range(NCH)]
        out_stored = [sem(f"out_stored{c}") for c in range(NCH)]
        dve_step, waited = sem("dve_step"), sem("waited")
        stats_ready, rstd_ready, xn_ready = sem("stats_ready"), sem("rstd_ready"), sem("xn_ready")
        pool_step = sem("pool_step")
        xnt_made, xnt_copied = sem("xnt_made"), sem("xnt_copied")
        mixed = sem("mixed")
        gate_made, gate_ready = sem("gate_made"), sem("gate_ready")
        k_made, k_relu, kact_ready = sem("k_made"), sem("k_relu"), sem("kact_ready")
        ffn_made, ffn_read, ffn_added = sem("ffn_made"), sem("ffn_read"), sem("ffn_added")
        q_made, kp_made, v_made = sem("q_made"), sem("kp_made"), sem("v_made")
        q_copied, kp_copied, squares = sem("q_copied"), sem("kp_copied"), sem("squares")
        rounded = sem("rounded")
        v_stored, q_split, k_split = sem("v_stored"), sem("q_split"), sem("k_split")
        q_saved, k_saved = sem("q_saved"), sem("k_saved")
        norms_made, norms_read = sem("norms_made"), sem("norms_read")
        bound_inputs, bound_ready, shift_ready, shift_saved = (
            sem("bound_inputs"), sem("bound_ready"), sem("shift_ready"), sem("shift_saved"))
        over_ready, over_counted, flag_ready = sem("over_ready"), sem("over_counted"), sem("flag_ready")
        pair_loaded = [sem(f"pair_loaded{i}") for i in range(2)]
        values_loaded = [sem(f"values_loaded{i}") for i in range(2)]
        ones_rows = sem("ones_rows")
        scored, exped, masked, summed, valued = sem("scored"), sem("exped"), sem("masked"), sem("summed"), sem("valued")
        y_copied, den_made, den_copied = sem("y_copied"), sem("den_made"), sem("den_copied")
        den_sent, den_back, rden_made, rden_sent, rden_back = (
            sem("den_sent"), sem("den_back"), sem("rden_made"), sem("rden_sent"), sem("rden_back"))
        y_scaled, bo_added, o_made, o_added = sem("y_scaled"), sem("bo_added"), sem("o_made"), sem("o_added")
        g_loaded, g_scored, g_read, g_max, g_sent, g_step = (
            sem("g_loaded"), sem("g_scored"), sem("g_read"), sem("g_max"), sem("g_sent"), sem("g_step"))

        def o_tile(blk):
            return banks[O_BANK[blk]][:, 0:C]

        LN_TURNS, FFN_TURNS = 3 * NCH, 2 * NCH
        V_TILES = NBLK * HEADS * LAT // CH

        V_ORDER = sorted(range(NCH), key=lambda c: c % 2)

        def v_tile(half, c, i):
            return half * NBLK + (V_ORDER.index(c) if half else c) * BPC + i

        V_BANK = [6 + t % 2 for t in range(NBLK)] + [(6, 7, 0, 1)[t % 4] for t in range(NBLK // 2)]
        V_BANK += [6 + t % 2 for t in range(NBLK // 2)]
        V_BEFORE = [max((u for u in range(t) if V_BANK[u] == V_BANK[t]), default=None) for t in range(2 * NBLK)]

        def ln(b, st, c):
            return b * LN_TURNS + (st * NCH + c)

        def ff(b, w, c):
            return b * FFN_TURNS + (w * NCH + c)

        def the_pair_before(pp):
            return nc.s_assert_within(pp * 2 - 1, 0, PAIRS - 1,
                                      skip_runtime_bounds_check_because="the first turn is left out")

        def wait_alone(eng, s, count):
            eng.wait_ge(s, count)
            eng.sem_inc(waited, 1)

        G_TURNS, G_STEPS = 2 * NBLK, 4
        g_part = sb("g_part", [P, NCH + 1])
        g_diag = probs[0][:, 0, 0:P]
        g_top = sb("g_top", [P, 1])
        g_shift = sb("g_shift", [P, 2, NBLK], bf16)

        def g_turn(b, p, i):
            return (b * PAIRS + p) * G_TURNS + i

        LOADS = 16 * (2 * len(PRODUCTS) + 1)

        block = ctx.enter_context(nc.Block())

        @block.sync
        def _(sp):
            for s, n in ((q_saved, 16), (k_saved, 16), (g_sent, 16), (den_sent, 48)):
                sp.sem_inc(s, n)
            def load_x0(c):
                rows = x[c * CH:(c + 1) * CH, :].rearrange("(n p) c -> p n c", p=P)
                sp.dma_start(x_sb[:, c * BPC:(c + 1) * BPC, :], rows).then_inc(x_loaded[c], 16)

            load_x0(0)
            sp.dma_start(wk_raw, wk_t).then_inc(wk_loaded, 16)
            sp.dma_start(b_k_raw[:], bk).then_inc(wk_loaded, 16)
            sp.wait_ge(wc_zeroed, 1)
            for i in range(2):
                sp.dma_start(wc_pair[i * LAT:(i + 1) * LAT, i * HD:(i + 1) * HD], wc_t).then_inc(wc_loaded, 16)
            load_x0(1)
            for dst, src in ((mur, mu_r), (muk, mu_k), (w_k, ffn_wk), (w_r, ffn_wr), (w_v, ffn_wv)):
                sp.dma_start(dst[:], src).then_inc(w_loaded, 16)
            for dst, src in ((wq_raw, wq), (wv_raw, wv)):
                sp.dma_start(dst, src).then_inc(raw_w_loaded, 16)
            for c in range(2, NCH):
                load_x0(c)
            sp.dma_start(b_q[:], bq).then_inc(bias_loaded, 16)
            sp.dma_start(b_val[:], bv.to_broadcast([P, HEADS * LAT])).then_inc(bias_loaded, 16)
            sp.dma_start(b_o[:], bo.to_broadcast([P, C])).then_inc(bias_loaded, 16)
            sp.dma_start(wo_raw, wo).then_inc(wo_raw_loaded, 16)
            sp.wait_ge(w_low, 2)
            sp.wait_ge(kc_copied, 3)
            sp.dma_start(wval_low_scratch, w_val_low[:].bitcast(fp32)).then_inc(low_there, 16)
            for i, low in enumerate((w_q_low, w_kc_low)):
                sp.dma_start(wqk_low_scratch[i], low[:].bitcast(fp32)).then_inc(low_there, 16)

            def part_rows(b, p, what, part):
                src = qk_scratch[b, what, part, bass.ds(p * (2 * HD), 2 * HD), :]
                return src.rearrange("(h d) t -> d h t", h=2)

            def load_pair(b, p, par):
                load_qk(b, p, par)
                load_values(p, par)

            def load_qk(b, p, par):
                for s, (qp, kp) in enumerate(PRODUCTS):
                    rows = slice(s * HD, (s + 1) * HD)
                    sp.dma_start(qs[par][rows, :, :], part_rows(b, p, 0, qp)).then_inc(pair_loaded[par], 16)
                    sp.dma_start(ks[par][rows, :, :], part_rows(b, p, 1, kp)).then_inc(pair_loaded[par], 16)
                src = shift_scratch[b, bass.ds(p * 2, 2), :].rearrange("(o h) t -> o h t", o=1)
                sp.dma_start(qs[par][QROWS - 1:QROWS, :, :], src).then_inc(pair_loaded[par], 16)

            def load_values(p, par):
                sp.dma_start(vb[par][:].rearrange("p a b -> p (a b)"),
                             slots[:, bass.ds(p, 1), :].rearrange("p o n -> p (o n)")).then_inc(values_loaded[par], 16)

            def reciprocals(n):
                for g in range(GROUPS):
                    sp.wait_ge(den_copied, n * GROUPS + (2 + g + 1))
                    sp.dma_start(den_scratch[g], den[0:P:32, g, :]).then_inc(den_sent, 16)
                sp.wait_ge(den_sent, n * (16 * GROUPS) + (16 * GROUPS + 48))
                spread = "g r (a c) -> (g r a) c"
                sp.dma_start(den_c[:], den_scratch.rearrange(spread, c=2 * T // P)).then_inc(den_back, 16)
                sp.wait_ge(rden_made, n + 1)
                sp.dma_start(rden_scratch.rearrange(spread, c=2 * T // P), rden_c[:]).then_inc(rden_sent, 16)
                sp.wait_ge(rden_sent, n * 16 + 16)
                sp.wait_ge(y_scaled, n + 1)
                for h in range(2):
                    src = rden_scratch.rearrange("g (c h) n -> h (g c) n", h=2)[h:h + 1]
                    sp.dma_start(rden[h * LAT:(h + 1) * LAT, :, :],
                                 src.to_broadcast([LAT, NCH, CH])).then_inc(rden_back, 16)

            def load_x(row, c):
                rows = x[bass.ds(row * T + c * CH, CH), :].rearrange("(n p) c -> p n c", p=P)
                sp.dma_start(x_sb[:, c * BPC:(c + 1) * BPC, :], rows).then_inc(x_loaded[c], 16)

            with sp.Fori(0, BATCH) as b:
                for c in range(NCH):
                    for what, parts, split, saved in ((0, q_parts, q_split, q_saved), (1, k_parts, k_split, k_saved)):
                        sp.wait_ge(split, b * NCH + (c + 1))
                        dst = qk_scratch[b, what, :, :, c * CH:(c + 1) * CH].rearrange("s (f p) t -> p (s f) t", p=P)
                        sp.dma_start(dst, parts.rearrange("p s f t -> p (s f) t")).then_inc(saved, 16)
                    if c == 0:
                        with sp.If(b < 1):
                            sp.wait_ge(wo_high_made, 1)
                            sp.wait_ge(wo_low_made, 1)
                            for i in range(2):
                                sp.dma_start(wo_scratch[i], wo_parts[i][:].bitcast(fp32)).then_inc(wo_saved, 16)
                sp.wait_ge(shift_ready, b + 1)
                sp.dma_start(shift_scratch[b], shift).then_inc(shift_saved, 16)
                wait_alone(sp, q_saved, b * (16 * NCH) + 16 * NCH + 16)
                wait_alone(sp, k_saved, b * (16 * NCH) + 16 * NCH + 16)
                wait_alone(sp, shift_saved, b * 16 + 16)
                wait_alone(sp, xnt_made, ln(b, 2, 0))
                wait_alone(sp, flag_ready, b + 1)
                general = sp.value_load(flag[0:1, 0:1], min_val=0, max_val=HEADS)
                with sp.If(general > 0):
                    with sp.Fori(0, PAIRS) as p:
                        for s, (qp, kp) in enumerate(PRODUCTS):
                            rows = slice(s * HD, (s + 1) * HD)
                            sp.dma_start(qs[0][rows, :, :], part_rows(b, p, 0, qp)).then_inc(g_loaded, 16)
                            sp.dma_start(ks[0][rows, :, :], part_rows(b, p, 1, kp)).then_inc(g_loaded, 16)
                        sp.wait_ge(g_max, b * PAIRS + p + 1)
                        dst = shift_scratch[b, bass.ds(p * 2, 2), :].rearrange("h (n p) -> p h n", p=P)
                        with nc.allow_non_contiguous_dma(reason="a column of maxima becomes a row"):
                            sp.dma_start(dst, g_shift[:]).then_inc(g_sent, 16)
                        wait_alone(sp, g_sent, (b * PAIRS + p) * 16 + 32)
                with sp.Else():
                    sp.sem_inc(g_loaded, PAIRS * len(PRODUCTS) * 32)
                    sp.sem_inc(g_sent, PAIRS * 16)
                load_qk(b, 0, 0)
                wait_alone(sp, v_stored, b * V_TILES + (V_TILES // 2 + 2 * BPC))
                load_values(0, 0)
                load_qk(b, 1, 1)
                wait_alone(sp, v_stored, b * V_TILES + V_TILES)
                load_values(1, 1)
                wait_alone(sp, low_there, b * 48 + 48)
                sp.wait_ge(wo_saved, 32)
                sp.dma_start(w_o[:].bitcast(fp32), wo_scratch[0]).then_inc(wo_loaded, 16)
                with sp.Fori(0, PAIRS // 2) as pp:
                    for par in range(2):
                        n = b * PAIRS + pp * 2 + par
                        wait_alone(sp, valued, n * NU + (NU + NP_BUF))
                        with sp.If(pp < PAIRS // 2 - 1):
                            later = nc.s_assert_within(pp * 2 + (par + 2), 0, PAIRS - 1,
                                                       skip_runtime_bounds_check_because="the last turn is left out")
                            load_pair(b, later, par)
                        if par == 0:
                            with sp.Else():
                                sp.dma_start(w_o_low[:].bitcast(fp32), wo_scratch[1]).then_inc(wo_loaded, 16)
                        reciprocals(n)
                for i, low in enumerate((w_q_low, w_kc_low)):
                    sp.dma_start(low[:].bitcast(fp32), wqk_low_scratch[i]).then_inc(low_there, 16)
                wait_alone(sp, o_made, b * NBLK + NBLK)
                sp.dma_start(w_val_low[:].bitcast(fp32), wval_low_scratch).then_inc(low_there, 16)
                for c in range(NCH):
                    sp.wait_ge(ffn_added, ff(b, 1, c) + 1)
                    rows = out[bass.ds(b * T + c * CH, CH), :].rearrange("(n p) c -> p n c", p=P)
                    sp.dma_start(rows, x_sb[:, c * BPC:(c + 1) * BPC, :]).then_inc(out_stored[c], 16)
                    wait_alone(sp, out_stored[c], b * 16 + 16)
                    with sp.If(b < BATCH - 1):
                        row = nc.s_assert_within(b + 1, 0, BATCH - 1,
                                                 skip_runtime_bounds_check_because="the last row is left out")
                        load_x(row, c)
            sp.wait_ge(rden_back, 32 * PAIRS * BATCH)
            sp.wait_ge(low_there, 48 * (BATCH + 1))

        @block.tensor
        def _(pe):
            mm = nc.tensor.matmul

            def transposes(b, st, c):
                pe.wait_ge(xn_ready, ln(b, st, c) + 1)
                pe.wait_ge(xnt_copied, ln(b, st, c) + 1)
                for ft in range(KT):
                    for i in range(BPC):
                        last = nc.tensor.transpose(pa[:, ft, i * P:(i + 1) * P], xn[c % 2][:, i, ft * P:(ft + 1) * P],
                                                   ident[:])
                last.then_inc(xnt_made, 1)

            def ffn(b, w):
                for c in range(NCH):
                    if w == 1 and c == NCH - 1:
                        with pe.If(b < BATCH - 1):
                            transposes(b + 1, 0, 0)
                    pe.wait_ge(mixed, ff(b, w, c) + 1 + 1)
                    pe.wait_ge(k_relu, ff(b, w, c) + 1)
                    if w == 1 and c == 0:
                        pe.wait_ge(o_added, b * NBLK + (2 * BPC + 2))
                    for mt in range(KT):
                        for kt in range(KT):
                            last = mm(pb[:, mt, :], w_k[:, kt, mt * P:(mt + 1) * P], x_k[c % 2][:, kt, :],
                                      start=kt == 0, stop=kt == KT - 1)
                    last.then_inc(k_made, 1)
                    pe.wait_ge(gate_ready, ff(b, w, c) + 1)
                    if w == 1 and c == 0:
                        pe.wait_ge(o_added, b * NBLK + NBLK)
                    for i in range(BPC):
                        for kt in range(KT):
                            last = mm(pc[:, i // 2, (i % 2) * C:(i % 2 + 1) * C], x_r[c % 2][:, kt, i * P:(i + 1) * P],
                                      w_r[:, kt, :], start=kt == 0, stop=kt == KT - 1)
                    last.then_inc(gate_made, 1)
                    if c + 2 < NCH:
                        transposes(b, 2 * w, c + 2)
                    elif w == 0:
                        transposes(b, 1, c + 2 - NCH)
                    elif c == NCH - 1:
                        with pe.If(b < BATCH - 1):
                            transposes(b + 1, 0, 1)
                    pe.wait_ge(kact_ready, ff(b, w, c) + 1)
                    pe.wait_ge(ffn_read, ff(b, w, c) + 1)
                    for i in range(BPC):
                        for kt in range(KT):
                            last = mm(pd[:, i // 2, (i % 2) * C:(i % 2 + 1) * C], kact[c % 2][:, kt, i * P:(i + 1) * P],
                                      w_v[:, kt, :], start=kt == 0, stop=kt == KT - 1)
                    last.then_inc(ffn_made, 1)

            def value_tile(b, half, c, i):
                tile = v_tile(half, c, i)
                if V_BEFORE[tile] is not None:
                    pe.wait_ge(v_stored, b * V_TILES + (V_BEFORE[tile] + 1))
                steps = [(kt, xs, ws) for kt in range(KT)
                         for xs, ws in ((x_high, w_val), (x_high, w_val_low), (x_low, w_val))]
                for k, (kt, xs, ws) in enumerate(steps):
                    last = mm(banks[V_BANK[tile]], xs[c][:, kt, i * P:(i + 1) * P],
                              ws[:, kt, half * CH:(half + 1) * CH], start=k == 0, stop=k == len(steps) - 1)
                last.then_inc(v_made, 1)

            def projections(b):
                for c in range(NCH):
                    turn = b * NCH + c
                    pe.wait_ge(xnt_copied, ln(b, 1, c) + 1 + 1)
                    for what, (dst, high, low, made) in enumerate(((pc, w_q, w_q_low, q_made),
                                                                   (pb, w_kc, w_kc_low, kp_made))):
                        if what == 0:
                            pe.wait_ge(*((q_copied, turn) if c else (gate_ready, ff(b, 0, NCH - 1) + 1 + 1)))
                        else:
                            pe.wait_ge(*((norms_read, turn) if c else (k_relu, ff(b, 0, NCH - 1) + 1 + 1)))
                        steps = [(kt, ws, xs) for kt in range(KT)
                                 for ws, xs in ((high, x_high), (high, x_low), (low, x_high))]
                        for mt in range(KT):
                            for k, (kt, ws, xs) in enumerate(steps):
                                last = mm(dst[:, mt, :], ws[:, kt, mt * P:(mt + 1) * P], xs[c][:, kt, :],
                                          start=k == 0, stop=k == len(steps) - 1)
                        last.then_inc(made, 1)
                        if c == 0 and what == 0:
                            pe.wait_ge(ffn_read, ff(b, 0, NCH - 1) + 1 + 1)
                        for i in range(2):
                            value_tile(b, 0, c, 2 * what + i)
                    pe.wait_ge(squares, turn * 2 + 2)
                    for what in range(2):
                        for ft in range(KT):
                            last = mm(pb[0:HEADS, what, :], head_rows[:, ft, :], sq[what][:, ft, :],
                                      start=ft == 0, stop=ft == KT - 1)
                    last.then_inc(norms_made, 1)
                    if c + 2 < NCH:
                        transposes(b, 1, c + 2)
                for c in V_ORDER:
                    for i in range(BPC):
                        value_tile(b, 1, c, i)
                    if c == 0:
                        pe.wait_ge(over_ready, b + 1)
                        wait_alone(pe, norms_read, (b + 1) * NCH)
                        mm(pb[0:1, 0, 0:1], over[:], ones[0:HEADS, 0:1], start=True, stop=True)\
                            .then_inc(over_counted, 1)

            def score(n, par, u):
                c, j, off, _ = UNITS[u]
                pe.wait_ge(exped, n * NU + (u + 1))
                for h in range(2):
                    last = mm(scores[u % 2][:, h, off:], ks[par][0:QROWS, h, j * P:(j + 1) * P],
                              qs[par][0:QROWS, h, c * CH + off:(c + 1) * CH], start=True, stop=True)
                last.then_inc(scored, 1)

            def value(n, par, u):
                c, j, off, diag = UNITS[u]
                if u in FIRST:
                    pe.wait_ge(y_copied, n * NCH + (c + 1))
                if diag:
                    pe.wait_ge(masked, n * NDIAG + (DIAG[u] + 1))
                else:
                    pe.wait_ge(exped, n * NU + (u + 2 + 1))
                for h in range(2):
                    last = mm(pc[h * LAT:(h + 1) * LAT, c % 2, off:], vb[par][:, j, h * LAT:(h + 1) * LAT],
                              probs[u % NP_BUF][:, h, off:], start=u in FIRST, stop=u in LAST)
                last.then_inc(valued, 1)

            def denominators(n, g):
                last_unit = LAST[2 * g + 1]
                pe.wait_ge(summed, n * NU + (last_unit + NP_BUF + 1))
                pe.wait_ge(den_copied, n * GROUPS + (g + 1))
                for r in range(4):
                    last = mm(pd[32 * r:32 * (r + 1), g, :], ones[:], acc[2 * g + r // 2][:, r % 2, :],
                              start=True, stop=True)
                last.then_inc(den_made, 1)

            pe.wait_ge(ident_set, 1)
            pe.sem_inc(valued, NP_BUF)
            pe.sem_inc(den_made, GROUPS)
            pe.wait_ge(wk_loaded, 32)
            pe.wait_ge(wc_loaded, 32)
            for p in range(PAIRS):
                if p == PAIRS // 2:
                    transposes(0, 0, 0)
                for ct in range(KT):
                    mm(pc[:, ct, p * 2 * HD:(p + 1) * 2 * HD], wk_raw[:, p, ct * P:(ct + 1) * P], wc_pair[:],
                       start=True, stop=True)
            per = P // (2 * HD)
            for p in range(PAIRS):
                r = p % per
                last = mm(pb[32 * r:32 * (r + 1), 0, p // per:p // per + 1], wc_pair[:], b_k_raw[:, p:p + 1],
                          start=True, stop=True)
            last.then_inc(kc_done, 1)
            pe.wait_ge(w_loaded, 16 * 5)
            pe.wait_ge(consts_set, 3)
            transposes(0, 0, 1)
            pe.wait_ge(kc_copied, 3)

            with pe.Fori(0, BATCH) as b:
                ffn(b, 0)
                wait_alone(pe, low_there, b * 48 + 48)
                projections(b)
                wait_alone(pe, flag_ready, b + 1)
                general = pe.value_load(flag[0:1, 0:1], min_val=0, max_val=HEADS)
                with pe.If(general > 0):
                    with pe.Fori(0, PAIRS) as p:
                        loads = len(PRODUCTS) * 32
                        wait_alone(pe, g_loaded, (b * PAIRS + p) * loads + loads)
                        for i in range(G_TURNS):
                            h, blk = divmod(i, NBLK)
                            pe.wait_ge(g_read, g_turn(b, p, i) + 1)
                            for k in range(blk // BPC + 1):
                                width = min(CH, (blk + 1) * P - k * CH)
                                last = mm(banks[k][:, 0:width], qs[0][0:QROWS - 1, h, blk * P:(blk + 1) * P],
                                          ks[0][0:QROWS - 1, h, k * CH:k * CH + width], start=True, stop=True)
                            last.then_inc(g_scored, 1)
                        wait_alone(pe, g_read, g_turn(b, p, G_TURNS) + 1)
                with pe.Else():
                    pe.sem_inc(g_scored, PAIRS * G_TURNS)
                wait_alone(pe, ones_rows, b * 2 + 1)
                def arrived(n_half, par):
                    pe.wait_ge(pair_loaded[par], n_half * LOADS + LOADS)

                arrived(b * (PAIRS // 2), 0)
                for u in range(PV_LAG):
                    score(b * PAIRS, 0, u)
                with pe.Fori(0, PAIRS // 2) as pp:
                    n0 = b * PAIRS + pp * 2
                    for v in range(2 * NU - PV_LAG):
                        if v % NU == 0:
                            pe.wait_ge(values_loaded[v // NU], (b * (PAIRS // 2) + pp) * 16 + 16)
                        value(n0 + v // NU, v // NU, v % NU)
                        s = v + PV_LAG
                        if s == NU:
                            arrived(b * (PAIRS // 2) + pp, 1)
                            wait_alone(pe, ones_rows, b * 2 + 2)
                        score(n0 + s // NU, s // NU, s % NU)
                        if v == 5:
                            with pe.If(pp > 0):
                                denominators(n0 - 1, GROUPS - 1)
                        if v % NU == LAST[1] + 2:
                            denominators(n0 + v // NU, 0)
                        if v == NU + 5:
                            denominators(n0, GROUPS - 1)
                    with pe.If(pp < PAIRS // 2 - 1):
                        arrived(b * (PAIRS // 2) + pp + 1, 0)
                        for k in range(PV_LAG):
                            value(n0 + 1, 1, NU - PV_LAG + k)
                            score(n0 + 2, 0, k)
                    with pe.Else():
                        for k in range(PV_LAG):
                            value(n0 + 1, 1, NU - PV_LAG + k)
                denominators(b * PAIRS + (PAIRS - 1), GROUPS - 1)
                pe.wait_ge(wo_loaded, b * 32 + 32)
                wait_alone(pe, exped, (b + 1) * (PAIRS * NU) + 2)
                for k, (first, end) in enumerate(O_PASSES):
                    for p in range(PAIRS):
                        pe.wait_ge(y_low_made, b * NYS + (Y_SPLITS.index((k, p)) + 1))
                        for blk in range(first, end):
                            if (k, p, blk) == (0, 0, 2):
                                wait_alone(pe, y_copied, (b + 1) * (PAIRS * NCH) + 2)
                            if (k, p, blk) == (0, 0, 4):
                                wait_alone(pe, den_copied, (b + 1) * (PAIRS * GROUPS) + 2)
                            if p == 0 and k > 0:
                                pe.wait_ge(o_added, b * NBLK + (O_BEFORE[blk] + 1))
                            at, cols = slice((blk - first) * P, (blk - first + 1) * P), slice(blk * P, (blk + 1) * P)
                            for i, (y, w) in enumerate(((y_high(k, p)[:, at], w_o), (y_high(k, p)[:, at], w_o_low),
                                                        (y_low[:, p, cols], w_o))):
                                last = mm(o_tile(blk), y, w[:, p, :], start=p == 0 and i == 0,
                                          stop=p == PAIRS - 1 and i == 2)
                            if p == PAIRS - 1:
                                last.then_inc(o_made, 1)
                        if (k, p) in ((1, PAIRS - 2), (2, PAIRS - 2)):
                            transposes(b, 2, k - 1)
                ffn(b, 1)

        @block.scalar
        def _(act):
            A = nc.scalar.activation

            def copy_xnt(b, st, c):
                act.wait_ge(xnt_made, ln(b, st, c) + 1)
                act.wait_ge(mixed, ff(b, st // 2, c) + 1 if st != 1 else ff(b, 1, 0) + 1)
                if st == 1:
                    A(x_high[c][:], pa[:], ACT.Copy).then_inc(x_high_made, 1)
                else:
                    A(xnt[c % 2][:, :, 1:CH + 1], pa[:], ACT.Copy).then_inc(xnt_copied, 1)

            def ffn(b, w):
                for c in range(NCH):
                    if w == 1 and c == NCH - 1:
                        with act.If(b < BATCH - 1):
                            copy_xnt(b + 1, 0, 0)
                    act.wait_ge(k_made, ff(b, w, c) + 1)
                    if c >= 2:
                        act.wait_ge(ffn_made, ff(b, w, c - 1))
                    A(kact[c % 2][:], pb[:], ACT.Relu).then_inc(k_relu, 1)
                    act.wait_ge(k_relu, ff(b, w, c) + 1 + 1)
                    A(kact[c % 2][:], kact[c % 2][:], ACT.Square).then_inc(kact_ready, 1)
                    if w == 0 and c == 2:
                        with act.If(b < 1):
                            act.wait_ge(wo_raw_loaded, 16)
                            A(wo_parts[0][:], wo_raw, ACT.Copy).then_inc(wo_high_made, 1)
                    act.wait_ge(gate_made, ff(b, w, c) + 1)
                    if c >= 2:
                        act.wait_ge(ffn_read, ff(b, w, c - 1) + 1)
                    A(gate[c % 2].rearrange("p (a b) c -> p a (b c)", a=2), pc[:], ACT.Sigmoid).then_inc(gate_ready, 1)
                    if c + 2 < NCH:
                        copy_xnt(b, 2 * w, c + 2)
                    elif w == 0:
                        copy_xnt(b, 1, c + 2 - NCH)
                    elif c == NCH - 1:
                        with act.If(b < BATCH - 1):
                            copy_xnt(b + 1, 0, 1)

            def y_copy(n, p, c):
                act.wait_ge(valued, n * NU + (LAST[c] + NP_BUF + 1))
                dst = slots[:, bass.ds(p, 1), c * CH:(c + 1) * CH].rearrange("p o n -> p (o n)")
                A(dst, pc[:, c % 2, :], ACT.Copy).then_inc(y_copied, 1)

            def den_copy(n, g):
                act.wait_ge(den_made, n * GROUPS + (g + GROUPS + 1))
                act.wait_ge(den_sent, n * (16 * GROUPS) + 48)
                A(den[:, g, :], pd[:, g, :], ACT.Copy).then_inc(den_copied, 1)

            for s in (xnt_copied, gate_ready, k_relu):
                act.sem_inc(s, 1)
            act.sem_inc(exped, 2)
            act.sem_inc(y_copied, 2)
            act.sem_inc(den_copied, 2)
            copy_xnt(0, 0, 0)
            act.wait_ge(kc_done, 1)
            A(w_kc[:], pc[:, :, 0:C], ACT.Copy).then_inc(kc_copied, 1)
            A(b_kc[:], pb[:, 0, 0:KT], ACT.Copy).then_inc(kc_copied, 1)
            act.wait_ge(kc_copied, 2)
            copy_xnt(0, 0, 1)
            act.wait_ge(raw_w_loaded, 32)
            A(w_q[:], wq_raw, ACT.Copy).then_inc(w_high, 1)
            A(w_val[:], wv_raw, ACT.Copy).then_inc(w_high, 1)

            with act.Fori(0, BATCH) as b:
                ffn(b, 0)
                act.wait_ge(bias_loaded, 16 * 3)
                for c in range(NCH):
                    turn = b * NCH + c
                    for what, (src, dst, bias, made, copied, high, saved) in enumerate((
                            (pc, qf, b_q, q_made, q_copied, q_parts, q_saved),
                            (pb, kf, b_kc, kp_made, kp_copied, k_parts, k_saved))):
                        act.wait_ge(made, turn + 1)
                        if c > 0:
                            act.wait_ge((q_split, k_split)[what], turn)
                        for mt in range(KT):
                            last = A(dst[:, mt, :], src[:, mt, :], ACT.Identity, bias=bias[:, mt:mt + 1])
                        last.then_inc(copied, 1)
                        act.wait_ge(copied, turn + 1)

                        def square():
                            if what == 0 and c > 0:
                                act.wait_ge(norms_made, turn)
                            elif what == 0:
                                act.wait_ge(ffn_read, ff(b, 1, 0) + 1)
                            A(sq[what], dst, ACT.Square).then_inc(squares, 1)

                        def round_high():
                            if c == 0:
                                act.wait_ge(ffn_added, ff(b, 1, 0))
                            act.wait_ge(saved, turn * 16 + 16)
                            A(high[:, 0], dst, ACT.Copy).then_inc(rounded, 1)

                        for step in (round_high, square) if what == 0 else (square, round_high):
                            step()
                    if c + 2 < NCH:
                        copy_xnt(b, 1, c + 2)

                def high_parts(b, splits):
                    for n, (k, p) in enumerate(splits):
                        first, end = O_PASSES[k]
                        if k == 1 and n and splits[n - 1][0] == 0:
                            act.wait_ge(summed, (b + 1) * (PAIRS * NU) + NP_BUF)
                        if k == 0:
                            act.wait_ge(y_scaled, b * PAIRS + (p + 1) + 1)
                        elif p == PAIRS - 1:
                            act.wait_ge(y_tail_scaled, b + 1)
                        A(y_high(k, p), slots[:, p, first * P:end * P], ACT.Copy).then_inc(y_high_made, 1)

                act.wait_ge(bound_inputs, b + 1)
                A(qnorm, qnorm, ACT.Sqrt, scale=row_max[:, 1:2]).then_inc(bound_ready, 1)
                A(exp_table[:], ident[0:1, 0:1], ACT.Exp)

                with act.Fori(0, PAIRS // 2) as pp:
                    n0 = b * PAIRS + pp * 2

                    for s in range(2 * NU):
                        par, u = divmod(s, NU)
                        n, off = n0 + par, UNITS[u][2]
                        act.wait_ge(scored, n * NU + (u + 1))
                        act.wait_ge(valued, n * NU + (u + 1))
                        act.wait_ge(summed, n * NU + (u + 1))
                        A(probs[u % NP_BUF][:, :, off:], scores[u % 2][:, :, off:], ACT.Exp,
                          scale=SCALE).then_inc(exped, 1)
                        for c in range(NCH - 1):
                            if u == LAST[c] + 4:
                                y_copy(n, pp * 2 + par, c)
                        if u == LAST[1] + 8:
                            den_copy(n, 0)
                        if s == 4:
                            with act.If(pp > 0):
                                y_copy(n0 - 1, the_pair_before(pp), NCH - 1)
                        if s == 9:
                            with act.If(pp > 0):
                                den_copy(n0 - 1, GROUPS - 1)
                        if s == NU + 4:
                            y_copy(n0, pp * 2, NCH - 1)
                        if s == NU + 9:
                            den_copy(n0, GROUPS - 1)
                high_parts(b, Y_SPLITS[:EARLY])
                y_copy(b * PAIRS + (PAIRS - 1), PAIRS - 1, NCH - 1)
                den_copy(b * PAIRS + (PAIRS - 1), GROUPS - 1)
                high_parts(b, Y_SPLITS[EARLY:])
                for c in range(2):
                    copy_xnt(b, 2, c)
                ffn(b, 1)

        @block.gpsimd
        def _(pool):
            g = nc.gpsimd
            g.memset(wc_pair[:], 0.0).then_inc(wc_zeroed, 1)
            pool.sem_inc(y_scaled, 1)
            g.memset(ident[:], 0.0).then_inc(pool_step, 1)
            g.memset(ones[:], 1.0).then_inc(consts_set, 1)
            g.memset(eps_half[:], -0.5).then_inc(pool_step, 1)
            g.memset(head_rows[:], 1.0).then_inc(pool_step, 1)
            g.memset(tri[:], 0.0).then_inc(pool_step, 1)
            pool.wait_ge(pool_step, 4)
            g.affine_select(out=ident[:], in_=ident[:], compare_op=ALU.not_equal, fill=1.0, base=0,
                            pattern=[[-1, P]], channel_multiplier=1).then_inc(ident_set, 1)
            g.affine_select(out=tri[:], in_=tri[:], compare_op=ALU.is_ge, fill=MASKED, base=0,
                            pattern=[[-1, P]], channel_multiplier=1).then_inc(consts_set, 1)
            hr = head_rows[:]
            g.affine_select(out=hr, in_=hr, compare_op=ALU.is_ge, fill=0.0, base=0,
                            pattern=[[P, KT], [-HD, HEADS]], channel_multiplier=1).then_inc(pool_step, 1)
            pool.wait_ge(pool_step, 5)
            g.affine_select(out=hr, in_=hr, compare_op=ALU.is_ge, fill=0.0, base=HD - 1,
                            pattern=[[-P, KT], [HD, HEADS]], channel_multiplier=-1).then_inc(consts_set, 1)

            def ln_power(b, st, c):
                turn = ln(b, st, c)
                wait_alone(pool, stats_ready, turn + 1)
                g.tensor_scalar(rstd[:, c % 2, :], mv[:, c % 2, :, 1], EPS, None, ALU.add).then_inc(pool_step, 1)
                pool.wait_ge(pool_step, turn + 6)
                g.tensor_tensor(rstd[:, c % 2, :], rstd[:, c % 2, :], eps_half[:], ALU.pow).then_inc(rstd_ready, 1)

            for c in range(2):
                ln_power(0, 0, c)
            pool.wait_ge(w_high, 2)
            for low, whole, high in ((w_q_low, wq_raw, w_q), (w_val_low, wv_raw, w_val)):
                g.tensor_tensor(low[:], whole, high[:].bitcast(fp32), ALU.subtract).then_inc(w_low, 1)
            with pool.Fori(0, BATCH) as b:
                for st in range(2):
                    for c in range(2 if st == 0 else 0, NCH):
                        ln_power(b, st, c)
                with pool.If(b < 1):
                    pool.wait_ge(wo_high_made, 1)
                    g.tensor_tensor(wo_parts[1][:], wo_raw, wo_parts[0][:].bitcast(fp32),
                                    ALU.subtract).then_inc(wo_low_made, 1)
                pool.wait_ge(xn_ready, ln(b, 1, NCH - 1) + 1)
                pool.wait_ge(wo_low_made, 1)
                pool.wait_ge(bias_loaded, 16 * 3)
                for i in range(NBLK):
                    g.tensor_tensor(x_sb[:, i, :], x_sb[:, i, :], b_o[:], ALU.add).then_inc(bo_added, 1)

                wait_alone(pool, k_saved, b * (16 * NCH) + 16 * NCH + 16)
                wait_alone(pool, q_saved, b * (16 * NCH) + 16 * NCH + 16)
                wait_alone(pool, bo_added, (b + 1) * NBLK)
                for i in range(2):
                    g.memset(ks[i][QROWS - 1:QROWS, :, :], 1.0).then_inc(ones_rows, 1)
                    wait_alone(pool, ones_rows, b * 2 + (i + 1))

                def scale_y(n, p):
                    pool.wait_ge(rden_back, n * 32 + 32)
                    pool.wait_ge(y_copied, n * NCH + (NCH + 2))
                    y = slots[:, bass.ds(p, 1), :].rearrange("p o n -> p (o n)")
                    g.tensor_tensor(y, y, rden[:].rearrange("p a b -> p (a b)"), ALU.mult).then_inc(y_scaled, 1)

                with pool.Fori(0, PAIRS // 2) as pp:
                    n0 = b * PAIRS + pp * 2
                    for par in range(2):
                        for u, (c, j, off, diag) in enumerate(UNITS):
                            if diag:
                                wait_alone(pool, exped, (n0 + par) * NU + (u + 3))
                                tile = probs[u % NP_BUF][:, :, off:off + P]
                                g.affine_select(out=tile, in_=tile, compare_op=ALU.is_ge, fill=0.0, base=0,
                                                pattern=[[0, 2], [1, P]], channel_multiplier=-1).then_inc(masked, 1)
                            if u == LAST[2]:
                                if par == 0:
                                    with pool.If(pp > 0):
                                        scale_y(n0 - 1, the_pair_before(pp))
                                else:
                                    scale_y(n0, pp * 2)
                last_pair = b * PAIRS + (PAIRS - 1)
                pool.wait_ge(rden_back, last_pair * 32 + 32)
                pool.wait_ge(y_copied, last_pair * NCH + (NCH + 2))
                tail = slice(O_PASSES[0][1] * P, NBLK * P)
                y = slots[:, PAIRS - 1, tail]
                g.tensor_tensor(y, y, rden[:].rearrange("p a b -> p (a b)")[:, tail], ALU.mult).then_inc(y_tail_scaled, 1)
                for c in range(NCH):
                    ln_power(b, 2, c)
                with pool.If(b < BATCH - 1):
                    for c in range(2):
                        ln_power(b + 1, 0, c)

        @block.vector
        def _(dve):
            v = nc.vector
            count = [0]

            def link(b, ins, alone=False):
                count[0] += 1
                ins.then_inc(dve_step, 1)
                (wait_alone if alone else type(dve).wait_ge)(dve, dve_step, b * STEPS + count[0])

            def ln_stats(b, st, c, ahead=False):
                if st == 0:
                    dve.wait_ge(x_loaded[c], b * 16 + 16)
                elif st == 1:
                    dve.wait_ge(ffn_added, ff(b, 0, c) + 1)
                else:
                    dve.wait_ge(o_added, b * NBLK + (c + 1) * BPC)
                for i in range(BPC):
                    last = v.bn_stats(stats[:, c % 2, i, :], x_sb[:, c * BPC + i, :])
                link(b - 1 if ahead else b, last, alone=True)
                for i in range(BPC):
                    last = v.bn_aggr(mv[:, c % 2, i, :], stats[:, c % 2, i, :])
                last.then_inc(stats_ready, 1)

            def ln_apply(b, st, c):
                turn = ln(b, st, c)
                dve.wait_ge(rstd_ready, turn + 1)
                if c >= 2 or st > 0:
                    dve.wait_ge(xnt_made, turn - 1)
                for i in range(BPC):
                    last = v.tensor_scalar(xn[c % 2][:, i, :], x_sb[:, c * BPC + i, :], mv[:, c % 2, i, 0:1],
                                           rstd[:, c % 2, i:i + 1], ALU.subtract, ALU.mult)
                last.then_inc(xn_ready, 1)

            def mix(b, w, c, ahead=False):
                cur, old = xnt[c % 2], xnt[(c + 1) % 2]
                now = b - 1 if ahead else b
                dve.wait_ge(xnt_copied, ln(b, 2 * w, c) + 1 + 1)
                if c == 0:
                    link(now, v.memset(cur[:, :, 0:1], 0.0))
                else:
                    link(now, v.tensor_copy(cur[:, :, 0:1], old[:, :, CH:CH + 1]))
                if c >= 2 or ahead:
                    dve.wait_ge(gate_made, ff(b, w, c - 1))
                link(now, v.tensor_tensor(diff, cur[:, :, 1:CH + 1], cur[:, :, 0:CH], ALU.subtract))
                for dst, mu in ((x_r, mur), (x_k, muk)):
                    for kt in range(KT):
                        last = v.scalar_tensor_tensor(dst[c % 2][:, kt, :], diff[:, kt, :], mu[:, kt:kt + 1],
                                                      cur[:, kt, 0:CH], ALU.mult, ALU.add)
                last.then_inc(mixed, 1)

            def add_ffn(b, w, c):
                dve.wait_ge(ffn_made, ff(b, w, c) + 1)
                dve.wait_ge(gate_ready, ff(b, w, c) + 1 + 1)
                if c > 0:
                    dve.wait_ge(ffn_added, ff(b, w, c))
                v.scalar_tensor_tensor(prod, pd[:].rearrange("p a (b c) -> p (a b) c", c=C), 0.5,
                                       gate[c % 2], ALU.mult, ALU.mult).then_inc(ffn_read, 1)
                dve.wait_ge(ffn_read, ff(b, w, c) + 1 + 1)
                xc = x_sb[:, c * BPC:(c + 1) * BPC, :]
                ins = v.tensor_tensor(xc, xc, prod, ALU.add)
                ins.then_inc(ffn_added, 1)

            def normalise(b, st, c, ahead=False):
                ln_stats(b, st, c, ahead)
                ln_apply(b, st, c)

            def ffn(b, w):
                normalise(b, 2 * w, 2)
                for c in range(NCH):
                    if c + 1 < NCH:
                        mix(b, w, c + 1)
                    if c + 3 < NCH:
                        normalise(b, 2 * w, c + 3)
                    elif w == 0:
                        normalise(b, 1, c + 3 - NCH)
                    elif c >= 2:
                        with dve.If(b < BATCH - 1):
                            normalise(b + 1, 0, c - 2, ahead=True)
                            if c == NCH - 1:
                                mix(b + 1, 0, 0, ahead=True)
                    if w == 0 and c >= 2:
                        lower(b, c - 2)
                    add_ffn(b, w, c)

            def lower(b, c):
                dve.wait_ge(x_high_made, b * NCH + (c + 1))
                v.tensor_tensor(x_low[c][:], pa[:], x_high[c][:].bitcast(fp32), ALU.subtract).then_inc(xnt_copied, 1)

            def store_v(b, half, c, i):
                tile, blk, per = v_tile(half, c, i), c * BPC + i, PAIRS // 2
                dve.wait_ge(v_made, b * V_TILES + (tile + 1))
                dst = slots[:, half * per:(half + 1) * per, blk * P:(blk + 1) * P]
                v.tensor_tensor(dst, banks[V_BANK[tile]].rearrange("p (a b) -> p a b", a=per),
                                b_val[:, half * CH:(half + 1) * CH].rearrange("p (a b) -> p a b", a=per),
                                ALU.add).then_inc(v_stored, 1)

            dve.sem_inc(summed, NP_BUF)
            for s in (ffn_read, mixed, g_read):
                dve.sem_inc(s, 1)
            normalise(0, 0, 0)
            normalise(0, 0, 1)
            dve.wait_ge(w_loaded, 16 * 5)
            dve.wait_ge(consts_set, 3)
            mix(0, 0, 0)
            dve.wait_ge(kc_copied, 2)
            v.tensor_tensor(w_kc_low[:], pc[:, :, 0:C], w_kc[:].bitcast(fp32), ALU.subtract).then_inc(kc_copied, 1)
            lead = count[0]
            with dve.Fori(0, BATCH) as b:
                ffn(b, 0)
                dve.wait_ge(bias_loaded, 16 * 3)
                for c in range(NCH):
                    turn = b * NCH + c
                    if c == 0:
                        ln_stats(b, 1, NCH - 1)
                    elif c == 1:
                        ln_apply(b, 1, NCH - 1)

                    def split(what):
                        src, parts, done = ((qf, q_parts, q_split), (kf, k_parts, k_split))[what]
                        dve.wait_ge(rounded, turn * 2 + (what + 1))
                        link(b, v.tensor_tensor(rest[what][:], src, parts[:, 0], ALU.subtract))
                        if what == 0:
                            store_v(b, 0, c, 1)
                        link(b, v.tensor_copy(parts[:, 1], rest[what][:]))
                        if what == 1 and c == NCH - 1:
                            store_v(b, 1, 0, 1)
                        v.tensor_tensor(parts[:, 2], rest[what][:], parts[:, 1], ALU.subtract).then_inc(done, 1)

                    store_v(b, 0, c, 0)
                    split(0)
                    for i in range(2, BPC):
                        store_v(b, 0, c, i)
                    dve.wait_ge(norms_made, turn + 1)
                    v.tensor_copy(qnorm[:, c * CH:(c + 1) * CH], pb[0:HEADS, 0, :])
                    v.tensor_reduce(norm_max[:, :, c:c + 1], pb[0:HEADS, :, :], AX.X, ALU.max).then_inc(norms_read, 1)
                    if c == NCH - 1:
                        dve.wait_ge(norms_read, (b + 1) * NCH)
                        v.tensor_reduce(row_max[:], norm_max[:], AX.X, ALU.max).then_inc(bound_inputs, 1)
                        dve.wait_ge(bound_inputs, b + 1)
                        link(b, v.tensor_tensor(over[:], row_max[:, 0:1], row_max[:, 1:2], ALU.mult))
                        v.tensor_scalar(over[:], over[:], SAFE ** 2, None, ALU.is_gt).then_inc(over_ready, 1)
                        dve.wait_ge(wo_saved, 32)
                        store_v(b, 1, 0, 0)
                    split(1)
                    if c + 2 < NCH:
                        lower(b, c + 2)
                dve.wait_ge(bound_ready, b + 1)
                v.tensor_scalar(shift, qnorm, -MARGIN, None, ALU.mult).then_inc(shift_ready, 1)
                for i in range(2, BPC):
                    store_v(b, 1, 0, i)
                dve.wait_ge(over_counted, b + 1)
                v.tensor_copy(flag[:], pb[0:1, 0, 0:1]).then_inc(flag_ready, 1)

                wait_alone(dve, flag_ready, b + 1)
                for c in V_ORDER[1:]:
                    for i in range(BPC):
                        store_v(b, 1, c, i)
                general = dve.value_load(flag[0:1, 0:1], min_val=0, max_val=HEADS)
                with dve.If(general > 0):
                    with dve.Fori(0, PAIRS) as p:
                        wait_alone(dve, g_sent, (b * PAIRS + p) * 16 + 16)
                        for i in range(G_TURNS):
                            h, blk = divmod(i, NBLK)
                            k, low = blk // BPC, blk % BPC * P
                            turn = g_turn(b, p, i)

                            def g_link(ins, step):
                                ins.then_inc(g_step, 1)
                                dve.wait_ge(g_step, turn * G_STEPS + step)

                            g_link(v.memset(g_part[:], MASKED), 1)
                            dve.wait_ge(g_scored, turn + 1)
                            for full in range(k):
                                v.tensor_reduce(g_part[:, full:full + 1], banks[full][:], AX.X, ALU.max)
                            if low:
                                v.tensor_reduce(g_part[:, k:k + 1], banks[k][:, 0:low], AX.X, ALU.max)
                            g_link(v.tensor_tensor(g_diag, banks[k][:, low:low + P], tri[:], ALU.add), 2)
                            g_link(v.tensor_reduce(g_part[:, NCH:NCH + 1], g_diag, AX.X, ALU.max), 3)
                            g_link(v.tensor_reduce(g_top[:], g_part[:], AX.X, ALU.max), 4)
                            last = v.tensor_scalar(g_shift[:, h, blk:blk + 1], g_top[:], -1.0, None, ALU.mult)
                            last.then_inc(g_read, 1)
                        dve.wait_ge(g_read, g_turn(b, p, G_TURNS) + 1)
                        dve.sem_inc(g_max, 1)
                with dve.Else():
                    dve.sem_inc(g_step, PAIRS * G_TURNS * G_STEPS)
                    dve.sem_inc(g_read, PAIRS * G_TURNS)
                    dve.sem_inc(g_max, PAIRS)

                def invert(n):
                    dve.wait_ge(den_back, n * 16 + 16)
                    v.reciprocal(rden_c[:], den_c[:]).then_inc(rden_made, 1)

                with dve.Fori(0, PAIRS // 2) as pp:
                    n0 = b * PAIRS + pp * 2
                    for par in range(2):
                        n = n0 + par
                        for u, (c, j, off, diag) in enumerate(UNITS):
                            if diag:
                                dve.wait_ge(masked, n * NDIAG + (DIAG[u] + 1))
                            else:
                                dve.wait_ge(exped, n * NU + (u + 3))
                            if u in FIRST:
                                dve.wait_ge(den_made, n * GROUPS + (c // 2 + 1))
                                v.tensor_copy(acc[c][:], probs[u % NP_BUF][:]).then_inc(summed, 1)
                            else:
                                dve.wait_ge(summed, n * NU + (u + NP_BUF))
                                a = acc[c][:, :, off:]
                                v.tensor_tensor(a, a, probs[u % NP_BUF][:, :, off:], ALU.add).then_inc(summed, 1)
                            if u == 16:
                                if par == 0:
                                    with dve.If(pp > 0):
                                        invert(n0 - 1)
                                else:
                                    invert(n0)

                def low_parts(b, start, end):
                    for n in range(start, end):
                        k, p = Y_SPLITS[n]
                        cols = slice(O_PASSES[k][0] * P, O_PASSES[k][1] * P)
                        dve.wait_ge(y_high_made, b * NYS + (n + 1))
                        v.tensor_tensor(y_low[:, p, cols], slots[:, p, cols], y_high(k, p).bitcast(fp32),
                                        ALU.subtract).then_inc(y_low_made, 1)

                before_adds = Y_SPLITS.index((0, PAIRS - 1)) + 1
                low_parts(b, 0, PAIRS // 2)
                invert(b * PAIRS + (PAIRS - 1))
                low_parts(b, PAIRS // 2, before_adds - 2)
                last_pair = b * PAIRS + (PAIRS - 1)
                dve.wait_ge(rden_back, last_pair * 32 + 32)
                dve.wait_ge(y_copied, last_pair * NCH + (NCH + 2))
                cols = slice(0, O_PASSES[0][1] * P)
                v.tensor_tensor(slots[:, PAIRS - 1, cols], slots[:, PAIRS - 1, cols],
                                rden[:].rearrange("p a b -> p (a b)")[:, cols], ALU.mult).then_inc(y_scaled, 1)
                low_parts(b, before_adds - 2, before_adds)
                dve.wait_ge(bo_added, (b + 1) * NBLK)
                for k, (first, end) in enumerate(O_PASSES):
                    for blk in range(first, end):
                        dve.wait_ge(o_made, b * NBLK + (blk + 1))
                        v.tensor_tensor(x_sb[:, blk, :], x_sb[:, blk, :], o_tile(blk), ALU.add).then_inc(o_added, 1)
                    if k == 0:
                        normalise(b, 2, 0)
                        low_parts(b, before_adds, NYS)
                    elif k == 1:
                        normalise(b, 2, 1)
                        mix(b, 1, 0)
                ffn(b, 1)
            assert count[0] == STEPS + lead, count[0] - lead


STEPS = 45
_IN = ["x", "ffn_wr", "ffn_wk", "ffn_wv", "mu_r", "mu_k", "wq", "bq", "wk_t", "bk", "wc_t", "wv", "bv", "wo", "bo"]


def _layout(inputs):
    import numpy as np
    a = {k.removeprefix("L0_"): np.asarray(v) for k, v in inputs.items()}

    def rows(w, n=128):
        return np.ascontiguousarray(w.reshape(-1, n, w.shape[-1]).transpose(1, 0, 2))

    def cols(v, n=128):
        return np.ascontiguousarray(v.reshape(-1, n).T)

    return {
        "x": a["attn_x"].reshape(-1, a["attn_x"].shape[-1]),
        "ffn_wr": rows(a["ffn_W_r"].T), "ffn_wk": rows(a["ffn_W_k"].T), "ffn_wv": rows(a["ffn_W_v"].T),
        "mu_r": cols(a["ffn_mu_r"]), "mu_k": cols(a["ffn_mu_k"]),
        "wq": rows(a["attn_Wq"]), "bq": cols(a["attn_bq"]),
        "wk_t": rows(a["attn_Wk"].T), "bk": cols(a["attn_bk"]), "wc_t": np.ascontiguousarray(a["attn_Wc"].T),
        "wv": rows(a["attn_Wv"]), "bv": a["attn_bv"].reshape(1, -1), "wo": rows(a["attn_Wo"]),
        "bo": a["attn_bo"].reshape(1, -1),
    }


def kernel(**inputs):
    import numpy as np
    import concourse.bacc as bacc
    from concourse.bass_utils import run_bass_kernel_spmd

    batch, t, c = inputs["L0_attn_x"].shape
    heads = 16
    arrays = {f"in_{k}": v for k, v in _layout(inputs).items()}
    nc = bacc.Bacc("TRN2", target_bir_lowering=False, num_devices=1)
    ins = [nc.dram_tensor(f"in_{k}", arrays[f"in_{k}"].shape, mybir.dt.from_np(arrays[f"in_{k}"].dtype),
                          kind="ExternalInput").ap() for k in _IN]
    out = nc.dram_tensor("out", (batch * t, c), mybir.dt.float32, kind="ExternalOutput").ap()
    qk = nc.dram_tensor("qk_scratch", (batch, 2, 3, c, t), mybir.dt.bfloat16, kind="Internal").ap()
    wqk_low = nc.dram_tensor("wqk_low_scratch", (2, 128, c // 128, c), mybir.dt.float32, kind="Internal").ap()
    wval_low = nc.dram_tensor("wval_low_scratch", (128, c // 128, heads * 64), mybir.dt.float32, kind="Internal").ap()
    wo_parts = nc.dram_tensor("wo_scratch", (2, 128, heads // 2, c), mybir.dt.float32, kind="Internal").ap()
    shift = nc.dram_tensor("shift_scratch", (batch, heads, t), mybir.dt.bfloat16, kind="Internal").ap()
    den = nc.dram_tensor("den_scratch", (2, 4, 512), mybir.dt.float32, kind="Internal").ap()
    rden = nc.dram_tensor("rden_scratch", (2, 4, 512), mybir.dt.float32, kind="Internal").ap()
    macaron_block(nc, ins[0], out, *ins[1:], qk, wqk_low, wval_low, wo_parts, shift, den, rden)
    r = run_bass_kernel_spmd(nc, [arrays], core_ids=[0])
    return np.asarray(r.results[0]["out"]).reshape(batch, t, c)
```
